# Optimizing a Trainium2 kernel written in Bass

```python
import numpy as np
import jax
import jax.numpy as jnp

def _softmax(x, axis=-1):
    return jax.nn.softmax(x, axis=axis)

def _gelu(x):
    return jax.nn.gelu(x, approximate=True)

def _silu(x):
    return jax.nn.silu(x)

def _sigmoid(x):
    return jax.nn.sigmoid(x)

def _layernorm(x, axis=-1, eps=1e-05):
    m = jnp.mean(x, axis=axis, keepdims=True)
    v = jnp.var(x, axis=axis, keepdims=True)
    return (x - m) / jnp.sqrt(v + eps)

def _scatter_add(tgt, idx, src, axis=0):
    return tgt.at[idx].add(src)

def _segment_sum(src, seg, n):
    return jax.ops.segment_sum(src, seg, n)
kernel_name = 'mk_flamingo_gated_d1_seqx_r8_c4bdaf'

def setup_inputs(seed: int=0):
    np.random.seed(seed)
    _w = jnp.asarray

    def _rec_inputs():
        import jax
        import jax.numpy as jnp
        _rk = jax.random.key(seed)
        x = -0.0003929 + 0.9999 * jax.random.normal(jax.random.fold_in(_rk, 1), (64, 64, 128), jnp.float32)
        _lenS = 64 - jax.random.randint(jax.random.fold_in(_rk, 7), (64,), 0, max(1, 64 // 4) + 1, jnp.int32)
        _lenS2 = 64 - jax.random.randint(jax.random.fold_in(_rk, 8), (64,), 0, max(1, 64 // 4) + 1, jnp.int32)
        _ctx_1024P = jax.random.normal(jax.random.fold_in(_rk, 11), (64, 16, 128), jnp.float32)
        _ctx_1024c = jax.random.dirichlet(jax.random.fold_in(_rk, 511), 0.3 * jnp.ones((16,), jnp.float32), (64, 64))
        _ctx_1024t = jnp.einsum('bsk,bkd->bsd', _ctx_1024c, _ctx_1024P)
        _ctx_1024t = _ctx_1024t * jax.lax.rsqrt(jnp.mean(jnp.square(_ctx_1024t)) + 1e-12) * 0.953939
        ctx_1024 = 2.81802e-05 + 1.00001 * (_ctx_1024t + 0.3 * jax.random.normal(jax.random.fold_in(_rk, 611), (64, 64, 128), jnp.float32))
        _g = jax.random.normal(jax.random.fold_in(_rk, 9001), (2, 1), jnp.float32)
        _g = jnp.sign(_g) * jnp.maximum(jnp.abs(_g), 1.0) + (_g == 0) * 1.0
        g_xattn = _g[0]
        g_ffn = _g[1]
        return (x, ctx_1024, g_xattn, g_ffn)
    x, ctx_1024, g_xattn, g_ffn = _rec_inputs()

    def _L0_xattn_setup():
        import jax, jax.numpy as jnp
        import numpy as np
        B, L, D = (4, 512, 128)
        key = jax.random.key(seed)
        k1, k2 = jax.random.split(key)
        Q = jax.random.normal(k1, (B, L, D), dtype=jnp.float32)
        K = jax.random.normal(k2, (B, L, D), dtype=jnp.float32)
        return {'Q': Q, 'K': K}
    _L0_xattn_all = _L0_xattn_setup()
    _L0_xattn_in = {k: v for k, v in _L0_xattn_all.items() if k in ()}
    del _L0_xattn_all

    def _L0_ffn_setup():
        import jax, jax.numpy as jnp
        import numpy as np
        D_MODEL = 128
        N_EXPERTS = 8
        TOP_K = 2
        HIDDEN = 4 * D_MODEL
        key = jax.random.key(seed)
        ks = jax.random.split(key, 6)
        B, S = (2, 256)
        x = jax.random.normal(ks[0], (B, S, D_MODEL), dtype=jnp.float32)
        shared_w1 = jax.random.normal(ks[1], (HIDDEN, D_MODEL), dtype=jnp.float32) * 0.02
        shared_w2 = jax.random.normal(ks[2], (D_MODEL, HIDDEN), dtype=jnp.float32) * 0.02
        experts_w1 = jax.random.normal(ks[3], (N_EXPERTS, HIDDEN, D_MODEL), dtype=jnp.float32) * 0.02
        experts_w2 = jax.random.normal(ks[4], (N_EXPERTS, D_MODEL, HIDDEN), dtype=jnp.float32) * 0.02
        gate_w = jax.random.normal(ks[5], (N_EXPERTS, D_MODEL), dtype=jnp.float32) * 0.02
        return {'x': x, 'shared_w1': shared_w1, 'shared_w2': shared_w2, 'experts_w1': experts_w1, 'experts_w2': experts_w2, 'gate_w': gate_w}
    _L0_ffn_all = _L0_ffn_setup()
    _L0_ffn_in = {k: v for k, v in _L0_ffn_all.items() if k in ('shared_w1', 'shared_w2', 'experts_w1', 'experts_w2', 'gate_w')}
    del _L0_ffn_all
    return {'x': x, 'ctx_1024': ctx_1024, 'g_xattn': g_xattn, 'g_ffn': g_ffn, 'L0_ffn_shared_w1': _L0_ffn_in['shared_w1'], 'L0_ffn_shared_w2': _L0_ffn_in['shared_w2'], 'L0_ffn_experts_w1': _L0_ffn_in['experts_w1'], 'L0_ffn_experts_w2': _L0_ffn_in['experts_w2'], 'L0_ffn_gate_w': _L0_ffn_in['gate_w']}

def reference(x, ctx_1024, g_xattn, g_ffn, L0_ffn_shared_w1, L0_ffn_shared_w2, L0_ffn_experts_w1, L0_ffn_experts_w2, L0_ffn_gate_w):
    import jax
    import jax.numpy as jnp

    def _L0_xattn_ref(Q, K):
        import jax, jax.numpy as jnp
        import numpy as np
        B, L, D = (4, 512, 128)
        scores = jnp.einsum('btd,bsd->bts', K, K)
        Lq = Q.shape[1]
        mask = jnp.tril(jnp.ones((Lq, Lq), dtype=scores.dtype))
        scores = scores * mask[None, :, :]
        Q_proj = jnp.einsum('bts,bsd->btd', scores, Q)
        return Q + Q_proj

    def _L0_ffn_ref(x, shared_w1, shared_w2, experts_w1, experts_w2, gate_w):
        import jax, jax.numpy as jnp
        import numpy as np
        D_MODEL = 128
        N_EXPERTS = 8
        TOP_K = 2
        HIDDEN = 4 * D_MODEL
        B, S, D = x.shape
        T = B * S
        x_flat = x.reshape(T, D)
        shared = jnp.einsum('td,dh->th', x_flat, shared_w1.T)
        shared = jnp.einsum('th,hd->td', jax.nn.silu(shared), shared_w2.T)
        gate_logits = x_flat @ gate_w.T
        top_k_gates, top_k_idx = jax.lax.top_k(gate_logits, TOP_K)
        top_k_gates = jax.nn.softmax(top_k_gates, axis=1)
        gates = jnp.zeros((T, N_EXPERTS), dtype=x.dtype)
        gates = gates.at[jnp.arange(T)[:, None], top_k_idx].set(top_k_gates)
        h = jnp.einsum('td,ehd->teh', x_flat, experts_w1)
        expert_out = jnp.einsum('teh,edh->ted', jax.nn.silu(h), experts_w2)
        selected = jnp.einsum('ted,te->td', expert_out, gates)
        return (shared + selected).reshape(B, S, D)
    x = x + jnp.tanh(g_xattn[0]) * _L0_xattn_ref(_layernorm(x, axis=-1), ctx_1024)
    x = x + jnp.tanh(g_ffn[0]) * _L0_ffn_ref(_layernorm(x, axis=-1), L0_ffn_shared_w1, L0_ffn_shared_w2, L0_ffn_experts_w1, L0_ffn_experts_w2, L0_ffn_gate_w)
    return x

_drawn_inputs = setup_inputs


def setup_inputs(seed=0):
    import zlib

    import numpy as np

    out = dict(_drawn_inputs(seed))
    spreads = {}
    factors = {'L0_ffn_shared_w1': 24.876,
     'L0_ffn_shared_w2': 21.879,
     'L0_ffn_experts_w1': 32.011,
     'L0_ffn_experts_w2': 28.559,
     'L0_ffn_gate_w': 32.069}
    for name, (base, spread) in spreads.items():
        noise = np.random.default_rng([zlib.crc32(name.encode()), seed]).standard_normal(out[name].shape)
        drawn = base * np.exp(spread * noise) if base else spread * noise
        out[name] = jnp.asarray(drawn.astype(out[name].dtype))
    for name, factor in factors.items():
        out[name] = (out[name] * factor).astype(out[name].dtype)
    return out
```

```python
import concourse.bass as bass
from concourse import mybir
from contextlib import ExitStack


def flamingo_gated_moe(nc, x, ctx, g_xattn, g_ffn, sw1, sw2, ew1, ew2, gate_w, out):
    f32 = mybir.dt.float32
    f32r = mybir.dt.float32r
    bf16 = mybir.dt.bfloat16
    i32 = mybir.dt.int32
    ALU = mybir.AluOpType
    ACT = mybir.ActivationFunctionType
    AX = mybir.AxisListType.X
    ds = bass.ds

    P = 128
    B, S, D = x.shape
    H = sw1.shape[0]
    E = gate_w.shape[0]
    K = 2
    T = B * S
    TILES = T // P
    HC = H // P
    G = 4
    GROUPS = TILES // G
    GW = G * D
    EPS = 1e-5
    BLOCKS = (K * T + E * (P - 1)) // P
    RING = 4
    BLOCKS = -(-BLOCKS // RING) * RING
    ROUNDS = BLOCKS // RING
    SHARED_PER_ROUND = 2
    SHARED_ROUNDS = TILES // SHARED_PER_ROUND
    TOKEN_SHIFT = T.bit_length() - 1
    P_SHIFT = P.bit_length() - 1
    FAR = -3.0e38

    x_rows = x.rearrange("b s d -> (b s) d").rearrange("(t p) d -> p t d", p=P)
    ctx_rows = ctx.rearrange("b s d -> (b s) d").rearrange("(t p) d -> p t d", p=P)
    out_rows = out.rearrange("b s d -> (b s) d").rearrange("(t p) d -> p t d", p=P)

    ew1_rows = ew1.rearrange("e (c p) d -> p (e c) d", p=P)
    ew2_rows = ew2.rearrange("e d h -> d e h")

    stack = ExitStack()
    with stack:
        def sb(name, shape, dt=f32):
            return stack.enter_context(nc.sbuf_tensor(name, shape, dt))

        def sem(name):
            return stack.enter_context(nc.semaphore(name))

        n_dram = nc.dram_tensor("n_rows", (T, D), f32, kind="Internal").ap()
        y_dram = nc.dram_tensor("y_rows", (K * T + BLOCKS * P, D), f32, kind="Internal").ap()
        n_rows = n_dram.rearrange("(t p) d -> p t d", p=P)
        y_by_choice = y_dram[0:K * T, :].rearrange("(k t p) d -> p k t d", p=P, k=K)

        xres = sb("xres", [P, TILES * D])
        nTH = sb("nTH", [D, T], f32r)
        nTL = sb("nTL", [D, T], f32r)
        w1H = sb("w1H", [D, (E + 1) * H], f32r)
        w1L = sb("w1L", [D, (E + 1) * H], f32r)
        w2H = sb("w2H", [P, (E + 1) * HC * D], f32r)
        w2L = sb("w2L", [P, (E + 1) * HC * D], f32r)
        w1_in = sb("w1_in", [P, (E + 1) * HC * D])
        w2_in = sb("w2_in", [D, (E + 1) * H])
        gate_in = sb("gate_in", [E, D])
        gTH = sb("gTH", [D, E], f32r)
        gTL = sb("gTL", [D, E], f32r)
        ident = sb("ident", [P, P])
        mask = sb("mask", [P, P])
        before = sb("before", [P, P], bf16)
        ones = sb("ones", [P, P], bf16)
        lane_row = sb("lane_row", [P, P], bf16)
        block_row = sb("block_row", [P, BLOCKS], bf16)
        block_start = sb("block_start", [1, BLOCKS])
        lane = sb("lane", [P, 1])
        pad_row = sb("pad_row", [P, BLOCKS])
        rev_expert = sb("rev_expert", [P, E])
        restart = sb("restart", [P, E * TILES])
        tanh_g = sb("tanh_g", [P, 2])
        ctx_in = sb("ctx_in", [P, 2, GW])
        stats = sb("stats", [P, 2, 2, G, 6])
        mv1 = sb("mv1", [P, 2, G, 2])
        rstd1 = sb("rstd1", [P, 2, G])
        mv2 = sb("mv2", [P, 2, G, 2])
        rstd2 = sb("rstd2", [P, 2, G])
        shift2 = sb("shift2", [P, 2, G])
        unused = sb("unused", [P, 1])
        minus_half = sb("minus_half", [P, G])
        neg_mean = sb("neg_mean", [P, 2, G])
        centred = sb("centred", [P, GW])
        q = sb("q", [P, 2, GW])
        kT = sb("kT", [D, 2, GW])
        scores = sb("scores", [P, 2, GW])
        n = sb("n", [P, 2, GW])
        cells = E * TILES
        spare = [t[:, j, c * cells:(c + 1) * cells] for t in (kT, scores) for j in range(2) for c in range(GW // cells)]
        logit, work, work2, *pick = (v.rearrange("p (t e) -> p t e", e=E) for v in spare[:3 + K])
        total, upto, where = (v.rearrange("p (e t) -> p e t", t=TILES) for v in spare[3 + K:6 + K])
        best = sb("best", [P, K, TILES])
        rank = sb("rank", [P, TILES])
        picked = sb("picked", [P, TILES, E], bf16)
        count_i = sb("count_i", [P, E], i32)
        padded = sb("padded", [P, E])
        upto_e = sb("upto_e", [P, E])
        ones_e = sb("ones_e", [P, E])
        start_e = sb("start_e", [P, E])
        passed = sb("passed", [1, BLOCKS, E])
        expert_f = sb("expert_f", [1, BLOCKS])
        weight_at = sb("weight_at", [1, BLOCKS], i32)
        slot = sb("slot", [P, K, TILES])
        slot_i = sb("slot_i", [P, K * TILES], i32)
        slot_lane_i = sb("slot_lane_i", [P, K * TILES], i32)
        slot_block_i = sb("slot_block_i", [P, K * TILES], i32)
        slot_lane = sb("slot_lane", [P, K * TILES])
        slot_block = sb("slot_block", [P, K * TILES])
        gate_e = sb("gate_e", [P, TILES])
        gate_d = sb("gate_d", [P, TILES])
        gates = sb("gates", [P, K, TILES])
        at_lane = sb("at_lane", [P, 4, P], bf16)
        at_block = sb("at_block", [P, 4, 2 * BLOCKS], bf16)
        inverse = sb("inverse", [P, 2 * BLOCKS])
        is_pad = sb("is_pad", [P, BLOCKS])
        dest_f = sb("dest_f", [P, BLOCKS])
        dest = sb("dest", [P, BLOCKS], i32)
        source = sb("source", [P, BLOCKS], i32)
        source_now = sb("source_now", [P, RING], i32)
        dest_now = sb("dest_now", [P, RING], i32)
        xTH = sb("xTH", [D, 2, P], f32r)
        xTL = sb("xTL", [D, 2, P], f32r)
        hTH = sb("hTH", [P, 2, HC * P], f32r)
        hTL = sb("hTL", [P, 2, HC * P], f32r)
        h = w2_in[:, 0:2 * H].rearrange("p (s h) -> p s h", s=2)
        rows_in = w2_in[:, 2 * H:2 * H + RING * D].rearrange("p (s d) -> p s d", s=RING)
        y = w2_in[:, 3 * H:3 * H + RING * D].rearrange("p (s d) -> p s d", s=RING)
        sT = w2_in[:, 4 * H:4 * H + HC * P]
        sTH = sb("sTH", [P, HC * P], f32r)
        sTL = sb("sTL", [P, HC * P], f32r)
        y_in = w1_in[:, 0:2 * K * GW].rearrange("p (j k d) -> p j k d", j=2, k=K)

        bank = [stack.enter_context(nc.psum_tensor(f"bank{i}", [P, 512], f32)) for i in range(8)]
        ps_k, ps_s, ps_q, ps_n, ps_logit = bank[0], bank[1], bank[2], bank[3], bank[4]
        ps_w = [bank[5], bank[6]]
        ps_before, ps_total, ps_inverse = bank[0], bank[1], bank[2]
        ps_x, ps_up, ps_hT, ps_y = bank[0], [bank[1], bank[2]], [bank[3], bank[4]], bank[5]
        ps_sup, ps_sy = bank[6], bank[7]

        pool_holds = sem("pool_holds")
        act_holds = sem("act_holds")
        dve_holds = sem("dve_holds")
        pe_holds = sem("pe_holds")
        consts_ready = sem("consts_ready")
        pool_steps = sem("pool_steps")
        small_in = sem("small_in")
        x_in = [sem(f"x_in{i}") for i in range(3)]
        ctx_loaded = [sem(f"ctx_loaded{j}") for j in range(2)]
        w_loaded = sem("w_loaded")
        tanh_done = sem("tanh_done")
        kT_psum = sem("kT_psum")
        kT_done = sem("kT_done")
        s_psum = sem("s_psum")
        scores_done = sem("scores_done")
        stats1_part = sem("stats1_part")
        stats1_done = sem("stats1_done")
        centred_done = sem("centred_done")
        q_done = sem("q_done")
        attn_psum = sem("attn_psum")
        x1_done = sem("x1_done")
        rstd1_part = sem("rstd1_part")
        rstd1_done = sem("rstd1_done")
        scale2_part = sem("scale2_part")
        scale2_done = sem("scale2_done")
        stats2_part = sem("stats2_part")
        stats2_done = sem("stats2_done")
        n_done = sem("n_done")
        n_stored = [sem(f"n_stored{j}") for j in range(2)]
        nT_psum = sem("nT_psum")
        nTH_done = sem("nTH_done")
        nTL_done = sem("nTL_done")
        gate_psum = sem("gate_psum")
        w_psum = sem("w_psum")
        wH_done = sem("wH_done")
        wL_done = sem("wL_done")
        logit_psum = sem("logit_psum")
        route = sem("route")
        gate_exp = sem("gate_exp")
        picked_done = sem("picked_done")
        prefix_psum = sem("prefix_psum")
        onehot_done = sem("onehot_done")
        onehot_used = sem("onehot_used")
        gate_gap_done = sem("gate_gap_done")
        tables_done = sem("tables_done")
        source_set = sem("source_set")
        dest_set = sem("dest_set")
        gathered = [sem(f"gathered{j}") for j in range(RING)]
        scattered = [sem(f"scattered{j}") for j in range(RING)]
        xT_psum = sem("xT_psum")
        xTH_done = sem("xTH_done")
        xTL_done = sem("xTL_done")
        up_psum = sem("up_psum")
        h_done = sem("h_done")
        hT_psum = sem("hT_psum")
        hTH_done = sem("hTH_done")
        hTL_done = sem("hTL_done")
        y_psum = sem("y_psum")
        y_done = sem("y_done")
        sup_psum = sem("sup_psum")
        sT_done = sem("sT_done")
        sTH_done = sem("sTH_done")
        sTL_done = sem("sTL_done")
        sy_psum = sem("sy_psum")
        shared_done = sem("shared_done")
        y_loaded = [sem(f"y_loaded{j}") for j in range(2)]
        half_done = sem("half_done")
        out_done = sem("out_done")
        stored = sem("stored")

        def at_least(eng, semaphore, value):
            if not (isinstance(value, int) and value <= 0):
                eng.wait_ge(semaphore, value)

        def hold(eng, counter):
            eng.sem_inc(counter, 1)

        def run_phase_a(eng, stages):
            s1, s2, s3 = stages
            last = GROUPS // 2 - 1
            s1(0, 0)
            s1(0, 1)
            s2(0, 0)
            with eng.Fori(1, GROUPS // 2) as qq:
                s1(qq, 0)
                s2(qq - 1, 1)
                s3(qq - 1, 0)
                s1(qq, 1)
                s2(qq, 0)
                s3(qq - 1, 1)
            s2(last, 1)
            s3(last, 0)
            s3(last, 1)

        block = stack.enter_context(nc.Block())

        @block.sync
        def _(sp):
            sp.dma_start(tanh_g[:, 0:1], g_xattn.rearrange("(a n) -> a n", a=1).to_broadcast([P, 1])).then_inc(small_in, 16)
            sp.dma_start(tanh_g[:, 1:2], g_ffn.rearrange("(a n) -> a n", a=1).to_broadcast([P, 1])).then_inc(small_in, 16)
            sp.dma_start(gate_in[:, :], gate_w).then_inc(small_in, 16)

            def load_ctx(qq, j):
                at_least(sp, kT_psum, 2 * qq + j - 1)
                sp.dma_start(ctx_in[:, j].rearrange("p (t d) -> p t d", d=D),
                             ctx_rows[:, ds((2 * qq + j) * G, G), :]).then_inc(ctx_loaded[j], 16)

            def store_n(qq, j):
                g = 2 * qq + j
                sp.wait_ge(n_done, G * (g + 1))
                sp.dma_start(n_rows[:, ds(g * G, G), :],
                             n[:, j].rearrange("p (t d) -> p t d", d=D)).then_inc(n_stored[j], 16)

            load_ctx(0, 0)
            for part, (a, b) in enumerate(((0, G), (G, 2 * G), (2 * G, TILES))):
                sp.dma_start(xres[:, a * D:b * D].rearrange("p (t d) -> p t d", d=D),
                             x_rows[:, a:b, :]).then_inc(x_in[part], 16)
                if part == 0:
                    load_ctx(0, 1)
            def load_experts(first, count):
                sp.dma_start(w1_in[:, ds(first * H, count * H)].rearrange("p (a d) -> p a d", d=D),
                             ew1_rows[:, ds(first * HC, count * HC), :]).then_inc(w_loaded, 16)
                sp.dma_start(w2_in[:, ds(first * H, count * H)].rearrange("p (e h) -> p e h", h=H),
                             ew2_rows[:, ds(first, count), :]).then_inc(w_loaded, 16)

            sp.dma_start(w1_in[:, E * H:].rearrange("p (c d) -> p c d", d=D),
                         sw1.rearrange("(c p) d -> p c d", p=P)).then_inc(w_loaded, 16)
            sp.dma_start(w2_in[:, E * H:], sw2).then_inc(w_loaded, 16)
            load_experts(0, 2)
            with sp.Fori(1, GROUPS // 2) as qq:
                for j in range(2):
                    load_ctx(qq, j)
                    store_n(qq - 1, j)
                load_experts(2 * qq, 2)
            store_n(GROUPS // 2 - 1, 0)
            store_n(GROUPS // 2 - 1, 1)

            for j in range(RING):
                sp.wait_ge(scattered[j], 16 * ROUNDS)

            def load_y(qq, j):
                at_least(sp, out_done, (2 * qq + j - 1) * G)
                for k in range(K):
                    sp.dma_start(y_in[:, j, k].rearrange("p (t d) -> p t d", d=D),
                                 y_by_choice[:, k, ds((2 * qq + j) * G, G), :]).then_inc(y_loaded[j], 16)

            def store_out(qq, j):
                g = 2 * qq + j
                sp.wait_ge(out_done, G * (g + 1))
                sp.dma_start(out_rows[:, ds(g * G, G), :],
                             xres[:, ds(g * GW, GW)].rearrange("p (t d) -> p t d", d=D)).then_inc(stored, 16)

            load_y(0, 0)
            load_y(0, 1)
            with sp.Fori(1, GROUPS // 2) as qq:
                for j in range(2):
                    load_y(qq, j)
                    store_out(qq - 1, j)
            store_out(GROUPS // 2 - 1, 0)
            store_out(GROUPS // 2 - 1, 1)
            sp.wait_ge(stored, 16 * GROUPS)

        @block.gpsimd
        def _(pool):
            counter = pool_holds
            step = [0]

            def chained(instruction):
                step[0] += 1
                instruction.then_inc(pool_steps, 1)
                pool.wait_ge(pool_steps, step[0])

            chained(pool.memset(ident[:, :], 0.0))
            chained(pool.affine_select(out=ident[:, :], in_=ident[:, :], compare_op=ALU.not_equal, fill=1.0,
                                       base=0, pattern=[[-1, P]], channel_multiplier=1))
            chained(pool.memset(mask[:, :], 1.0))
            chained(pool.affine_select(out=mask[:, :], in_=mask[:, :], compare_op=ALU.is_ge, fill=0.0,
                                       base=0, pattern=[[1, P]], channel_multiplier=-1))
            chained(pool.affine_select(out=mask[:, S:P], in_=mask[:, S:P], compare_op=ALU.is_ge, fill=0.0,
                                       base=-S, pattern=[[0, P - S]], channel_multiplier=1))
            chained(pool.memset(before[:, :], 1.0))
            chained(pool.affine_select(out=before[:, :], in_=before[:, :], compare_op=ALU.is_gt, fill=0.0,
                                       base=0, pattern=[[1, P]], channel_multiplier=-1))
            chained(pool.memset(ones[:, :], 1.0))
            chained(pool.memset(ones_e[:, :], 1.0))
            chained(pool.memset(minus_half[:, :], -0.5))
            chained(pool.iota(lane_row[:, :], pattern=[[1, P]], base=0, channel_multiplier=0,
                              allow_small_or_imprecise_dtypes=True))
            chained(pool.iota(block_row[:, :], pattern=[[1, BLOCKS]], base=0, channel_multiplier=0,
                              allow_small_or_imprecise_dtypes=True))
            chained(pool.iota(block_start[:, :], pattern=[[P, BLOCKS]], base=0, channel_multiplier=0,
                              allow_small_or_imprecise_dtypes=True))
            chained(pool.iota(lane[:, :], pattern=[[0, 1]], base=0, channel_multiplier=1,
                              allow_small_or_imprecise_dtypes=True))
            chained(pool.iota(pad_row[:, :], pattern=[[P, BLOCKS]], base=K * T + P, channel_multiplier=1,
                              allow_small_or_imprecise_dtypes=True))
            chained(pool.iota(rev_expert[:, :], pattern=[[-1, E]], base=E, channel_multiplier=0,
                              allow_small_or_imprecise_dtypes=True))
            chained(pool.memset(restart[:, :], 1.0))
            chained(pool.memset(restart[:, :].rearrange("p (e t) -> p e t", t=TILES)[:, :, 0:1], 0.0))
            pool.memset(unused[:, :], 0.0).then_inc(consts_ready, 1)

            def centre_and_scale(qq, j):
                g = 2 * qq + j
                xg = xres[:, ds(g * GW, GW)].rearrange("p (t d) -> p t d", d=D)
                at_least(pool, attn_psum, g - 1)
                pool.wait_ge(stats1_done, g + 1)
                hold(pool, counter)
                pool.tensor_scalar(rstd1[:, j], mv1[:, j, :, 1], EPS, None, ALU.add).then_inc(rstd1_part, 1)
                pool.wait_ge(rstd1_part, g + 1)
                pool.tensor_tensor(rstd1[:, j], rstd1[:, j], minus_half[:, :], ALU.pow).then_inc(rstd1_done, 1)
                pool.tensor_tensor(centred[:, :].rearrange("p (t d) -> p t d", d=D), xg,
                                   mv1[:, j, :, 0:1].to_broadcast([P, G, D]), ALU.subtract).then_inc(centred_done, 1)
                pool.wait_ge(rstd1_done, g + 1)
                hold(pool, counter)
                pool.wait_ge(centred_done, g + 1)
                pool.tensor_tensor(q[:, j].rearrange("p (t d) -> p t d", d=D),
                                   centred[:, :].rearrange("p (t d) -> p t d", d=D),
                                   rstd1[:, j].unsqueeze(2).to_broadcast([P, G, D]), ALU.mult).then_inc(q_done, 1)

            def scale_and_shift(qq, j):
                g = 2 * qq + j
                at_least(pool, n_done, G * (g - 1))
                hold(pool, counter)
                pool.wait_ge(stats2_done, g + 1)
                hold(pool, counter)
                pool.tensor_scalar(rstd2[:, j], mv2[:, j, :, 1], EPS, None, ALU.add).then_inc(scale2_part, 1)
                pool.tensor_scalar(neg_mean[:, j], mv2[:, j, :, 0], -1.0, None, ALU.mult).then_inc(scale2_part, 1)
                pool.wait_ge(scale2_part, 3 * g + 2)
                pool.tensor_tensor(rstd2[:, j], rstd2[:, j], minus_half[:, :], ALU.pow).then_inc(scale2_part, 1)
                pool.wait_ge(scale2_part, 3 * g + 3)
                pool.tensor_tensor(shift2[:, j], neg_mean[:, j], rstd2[:, j], ALU.mult).then_inc(scale2_done, 1)

            run_phase_a(pool, (centre_and_scale, scale_and_shift, lambda qq, j: None))

            def gather(r, j):
                b = RING * r + j
                pool.wait_ge(source_set, b + 1)
                hold(pool, counter)
                if not (isinstance(b, int) and b < RING):
                    pool.wait_ge(xT_psum, b - RING + 1)
                    hold(pool, counter)
                pool.indirect_dma_start(out=rows_in[:, j], out_offset=None, in_=n_dram[:, :],
                                        in_offset=bass.IndirectOffsetOnAxis(ap=source_now[:, j:j + 1], axis=0))\
                    .then_inc(gathered[j], 16)

            def scatter(r, j):
                b = RING * r + j
                pool.wait_ge(y_done, b + 1)
                hold(pool, counter)
                pool.indirect_dma_start(out=y_dram[:, :],
                                        out_offset=bass.IndirectOffsetOnAxis(ap=dest_now[:, j:j + 1], axis=0),
                                        in_=y[:, j], in_offset=None).then_inc(scattered[j], 16)

            pool.wait_ge(w_psum, 2 * (E + 1))
            for j in range(2):
                pool.wait_ge(n_stored[j], 16 * (GROUPS // 2))
            for j in range(RING):
                gather(0, j)
            with pool.Fori(1, ROUNDS) as r:
                for j in range(RING):
                    gather(r, j)
                    scatter(r - 1, j)
            for j in range(RING):
                scatter(ROUNDS - 1, j)

        @block.scalar
        def _(act):
            counter = act_holds
            act.preload_act_table(ACT.Silu)
            act.wait_ge(small_in, 48)
            act.activation(tanh_g[:, :], tanh_g[:, :], ACT.Tanh).then_inc(tanh_done, 1)

            def evacuate_kT(qq, j):
                g = 2 * qq + j
                at_least(act, s_psum, g - 1)
                act.wait_ge(kT_psum, g + 1)
                act.activation(kT[:, j], ps_k[:, :], ACT.Copy).then_inc(kT_done, 1)

            def normalise(qq, j):
                g = 2 * qq + j
                at_least(act, n_stored[j], 16 * qq)
                at_least(act, nT_psum, g - 1)
                act.wait_ge(scale2_done, g + 1)
                hold(act, counter)
                for t in range(G):
                    act.activation(n[:, j, t * D:(t + 1) * D], xres[:, ds(g * GW + t * D, D)], ACT.Identity,
                                   bias=shift2[:, j, t:t + 1], scale=rstd2[:, j, t:t + 1]).then_inc(n_done, 1)

            def high_part_nT(qq, j):
                g = 2 * qq + j
                act.wait_ge(nT_psum, g + 1)
                hold(act, counter)
                act.activation(nTH[:, ds(g * GW, GW)], ps_n[:, :], ACT.Copy).then_inc(nTH_done, 1)

            run_phase_a(act, (evacuate_kT, normalise, high_part_nT))

            for i in range(2 * (E + 1)):
                act.wait_ge(w_psum, i + 1)
                w = (w1H, w2H)[i % 2]
                act.activation(w[:, (i // 2) * H:(i // 2 + 1) * H], ps_w[i % 2][:, :], ACT.Copy).then_inc(wH_done, 1)

            act.wait_ge(gate_gap_done, 1)
            act.activation(gate_e[:, :], gate_d[:, :], ACT.Exp).then_inc(gate_exp, 1)
            act.preload_act_table(ACT.Silu)

            def high_part_xT(b, slot2):
                act.wait_ge(xT_psum, b + 1)
                at_least(act, up_psum, b - 1)
                act.activation(xTH[:, slot2], ps_x[:, 0:P], ACT.Copy).then_inc(xTH_done, 1)

            def silu(b, slot2):
                act.wait_ge(up_psum, b + 1)
                at_least(act, hT_psum, b - 1)
                act.activation(h[:, slot2], ps_up[slot2][:, :], ACT.Silu).then_inc(h_done, 1)

            def high_part_hT(b, slot2):
                act.wait_ge(hT_psum, b + 1)
                at_least(act, y_psum, b - 1)
                act.activation(hTH[:, slot2], ps_hT[slot2][:, :], ACT.Copy).then_inc(hTH_done, 1)

            def shared_silu(s):
                act.wait_ge(sup_psum, s + 1)
                at_least(act, sTL_done, s)
                act.activation(sT[:, :], ps_sup[:, :], ACT.Silu).then_inc(sT_done, 1)

            def act_round(r, shared, last=False):
                for j in range(RING):
                    b = RING * r + j
                    if not (last and j + 2 >= RING):
                        high_part_xT(b + 2, j % 2)
                    if not (last and j + 1 >= RING):
                        silu(b + 1, (j + 1) % 2)
                    high_part_hT(b, j % 2)
                    if shared and j % 2 == 0:
                        shared_silu(SHARED_PER_ROUND * r + j // 2)

            high_part_xT(0, 0)
            high_part_xT(1, 1)
            silu(0, 0)
            act_round(0, True)
            with act.Fori(1, SHARED_ROUNDS) as r:
                act_round(r, True)
            with act.Fori(SHARED_ROUNDS, ROUNDS - 1) as r:
                act_round(r, False)
            act_round(ROUNDS - 1, False, last=True)

        @block.vector
        def _(dve):
            counter = dve_holds
            step = [0]

            def chained(instruction):
                step[0] += 1
                instruction.then_inc(route, 1)
                dve.wait_ge(route, step[0])

            dve.wait_ge(consts_ready, 1)
            dve.wait_ge(tanh_done, 1)

            def mean_variance(src, mv, which, j, part, before_parts):
                for t in range(G):
                    dve.bn_stats(stats[:, which, j, t, :], src(t)).then_inc(part, 1)
                dve.wait_ge(part, before_parts + G)
                hold(dve, counter)
                for t in range(G):
                    last = dve.bn_aggr(mv[:, j, t, :], stats[:, which, j, t, :])
                return last

            def attend(qq, j):
                g = 2 * qq + j
                if isinstance(qq, int):
                    dve.wait_ge(x_in[j], 16)
                else:
                    dve.wait_ge(x_in[2], 16)
                at_least(dve, q_done, g - 1)
                hold(dve, counter)
                mean_variance(lambda t: xres[:, ds(g * GW + t * D, D)], mv1, 0, j, stats1_part, G * g)\
                    .then_inc(stats1_done, 1)
                at_least(dve, attn_psum, g - 1)
                dve.wait_ge(s_psum, g + 1)
                dve.tensor_tensor(scores[:, j].rearrange("p (t d) -> p t d", d=P),
                                  ps_s[:, :].rearrange("p (t d) -> p t d", d=P),
                                  mask[:, :].unsqueeze(1).to_broadcast([P, G, P]), ALU.mult).then_inc(scores_done, 1)

            def residual(qq, j):
                g = 2 * qq + j
                dve.wait_ge(attn_psum, g + 1)
                dve.scalar_tensor_tensor(out=xres[:, ds(g * GW, GW)], in0=ps_q[:, :], scalar=tanh_g[:, 0:1],
                                         in1=xres[:, ds(g * GW, GW)], op0=ALU.mult, op1=ALU.add).then_inc(x1_done, 1)
                dve.wait_ge(x1_done, g + 1)
                hold(dve, counter)
                at_least(dve, n_done, G * (g - 1))
                hold(dve, counter)
                mean_variance(lambda t: xres[:, ds(g * GW + t * D, D)], mv2, 1, j, stats2_part, G * g)\
                    .then_inc(stats2_done, 1)

            def low_part_nT(qq, j):
                g = 2 * qq + j
                dve.wait_ge(nTH_done, g + 1)
                dve.tensor_tensor(nTL[:, ds(g * GW, GW)], ps_n[:, :], nTH[:, ds(g * GW, GW)].bitcast(f32),
                                  ALU.subtract).then_inc(nTL_done, 1)

            run_phase_a(dve, (attend, residual, low_part_nT))

            dve.wait_ge(gate_psum, 1)
            chained(dve.tensor_copy(gTH[:, :], ps_k[:, 0:E]))
            chained(dve.tensor_tensor(gTL[:, :], ps_k[:, 0:E], gTH[:, :].bitcast(f32), ALU.subtract))
            gate_split = step[0]

            for i in range(2 * (E + 1)):
                dve.wait_ge(wH_done, i + 1)
                high, low = ((w1H, w1L), (w2H, w2L))[i % 2]
                cols = slice((i // 2) * H, (i // 2 + 1) * H)
                dve.tensor_tensor(low[:, cols], ps_w[i % 2][:, :], high[:, cols].bitcast(f32), ALU.subtract)\
                    .then_inc(wL_done, 1)

            dve.wait_ge(logit_psum, 1)
            chained(dve.tensor_copy(logit[:, :, :], ps_logit[:, 0:TILES * E].rearrange("p (t e) -> p t e", e=E)))
            rev = rev_expert[:, :].unsqueeze(1).to_broadcast([P, TILES, E])
            left = logit
            for k in range(K):
                top = best[:, k].unsqueeze(2)
                chained(dve.tensor_reduce(best[:, k], left[:, :, :], AX, ALU.max))
                chained(dve.tensor_tensor(work[:, :, :], left[:, :, :], top.to_broadcast([P, TILES, E]), ALU.is_equal))
                chained(dve.tensor_tensor(work[:, :, :], work[:, :, :], rev, ALU.mult))
                chained(dve.tensor_reduce(rank[:, :], work[:, :, :], AX, ALU.max))
                chained(dve.tensor_tensor(pick[k][:, :, :], rank[:, :].unsqueeze(2).to_broadcast([P, TILES, E]), rev,
                                          ALU.is_equal))
                if k == 0:
                    chained(dve.scalar_tensor_tensor(out=work2[:, :, :], in0=pick[0][:, :, :], scalar=FAR,
                                                     in1=logit[:, :, :], op0=ALU.mult, op1=ALU.add))
                    left = work2
            dve.tensor_tensor(gate_d[:, :], best[:, 1], best[:, 0], ALU.subtract).then_inc(gate_gap_done, 1)
            dve.tensor_tensor(picked[:, :, :], pick[0][:, :, :], pick[1][:, :, :], ALU.add).then_inc(picked_done, 1)
            dve.wait_ge(prefix_psum, 1)
            by_expert = "p (e t) -> p e t"
            cells = E * TILES
            chained(dve.tensor_copy(total[:, :, :], ps_total[:, 0:cells].rearrange(by_expert, t=TILES)))
            chained(dve.tensor_tensor_scan(upto[:, :, :].rearrange("p e t -> p (e t)"), restart[:, :],
                                           total[:, :, :].rearrange("p e t -> p (e t)"), 0.0, ALU.mult, ALU.add))
            chained(dve.tensor_scalar(count_i[:, :], upto[:, :, TILES - 1], float(P - 1), None, ALU.add))
            chained(dve.tensor_scalar(count_i[:, :], count_i[:, :], P_SHIFT, P_SHIFT, ALU.logical_shift_right,
                                      ALU.logical_shift_left))
            chained(dve.tensor_copy(padded[:, :], count_i[:, :]))
            chained(dve.tensor_tensor_scan(upto_e[:, :], ones_e[:, :], padded[:, :], 0.0, ALU.mult, ALU.add))
            chained(dve.tensor_tensor(start_e[:, :], upto_e[:, :], padded[:, :], ALU.subtract))
            chained(dve.tensor_tensor(passed[:, :, :], upto_e[0:1, :].unsqueeze(1).to_broadcast([1, BLOCKS, E]),
                                      block_start[:, :].unsqueeze(2).to_broadcast([1, BLOCKS, E]), ALU.is_le))
            chained(dve.tensor_reduce(expert_f[:, :], passed[:, :, :], AX, ALU.add))
            chained(dve.tensor_scalar(weight_at[:, :], expert_f[:, :], float(E - 1), float(H), ALU.min, ALU.mult))
            chained(dve.tensor_tensor(where[:, :, :], upto[:, :, :], total[:, :, :], ALU.subtract))
            chained(dve.tensor_tensor(where[:, :, :], where[:, :, :],
                                      start_e[:, :].unsqueeze(2).to_broadcast([P, E, TILES]), ALU.add))
            chained(dve.tensor_tensor(where[:, :, :], where[:, :, :],
                                      ps_before[:, 0:cells].rearrange(by_expert, t=TILES), ALU.add))
            for k in range(K):
                chained(dve.tensor_tensor(work[:, :, :], where[:, :, :].rearrange("p e t -> p t e"), pick[k][:, :, :],
                                          ALU.mult))
                chained(dve.tensor_reduce(slot[:, k], work[:, :, :], AX, ALU.add))
            chained(dve.tensor_copy(slot_i[:, :], slot[:, :, :].rearrange("p k t -> p (k t)")))
            chained(dve.tensor_scalar(slot_lane_i[:, :], slot_i[:, :], P - 1, None, ALU.bitwise_and))
            chained(dve.tensor_scalar(slot_block_i[:, :], slot_i[:, :], P_SHIFT, None, ALU.logical_shift_right))
            chained(dve.tensor_copy(slot_lane[:, :], slot_lane_i[:, :]))
            chained(dve.tensor_copy(slot_block[:, :], slot_block_i[:, :]))
            for i in range(K * TILES):
                s4 = i % 4
                at_least(dve, onehot_used, i - 3)
                dve.tensor_scalar(at_lane[:, s4], lane_row[:, :], slot_lane[:, i:i + 1], None, ALU.is_equal)\
                    .then_inc(onehot_done, 1)
                dve.tensor_scalar(at_block[:, s4, 0:BLOCKS], block_row[:, :], slot_block[:, i:i + 1], float(i + 1),
                                  ALU.is_equal, ALU.mult).then_inc(onehot_done, 1)
                dve.tensor_scalar(at_block[:, s4, BLOCKS:], block_row[:, :], slot_block[:, i:i + 1], lane[:, 0:1],
                                  ALU.is_equal, ALU.mult).then_inc(onehot_done, 1)
            dve.wait_ge(onehot_used, K * TILES)
            chained(dve.tensor_copy(inverse[:, :], ps_inverse[:, 0:2 * BLOCKS]))
            chained(dve.scalar_tensor_tensor(out=dest_f[:, :], in0=inverse[:, 0:BLOCKS], scalar=float(P),
                                             in1=inverse[:, BLOCKS:], op0=ALU.mult, op1=ALU.add))
            chained(dve.scalar_tensor_tensor(out=is_pad[:, :], in0=inverse[:, 0:BLOCKS], scalar=0.0,
                                             in1=pad_row[:, :], op0=ALU.is_equal, op1=ALU.mult))
            chained(dve.scalar_tensor_tensor(out=dest[:, :], in0=dest_f[:, :], scalar=-float(P), in1=is_pad[:, :],
                                             op0=ALU.add, op1=ALU.add))
            chained(dve.tensor_scalar(source[:, :], dest[:, :], T - 1, None, ALU.bitwise_and))
            dve.wait_ge(gate_exp, 1)
            chained(dve.tensor_scalar(gate_d[:, :], gate_e[:, :], 1.0, None, ALU.add))
            chained(dve.reciprocal(gates[:, 0], gate_d[:, :]))
            chained(dve.tensor_tensor(gates[:, 1], gates[:, 0], gate_e[:, :], ALU.mult))
            dve.tensor_scalar(gates[:, :, :], gates[:, :, :], tanh_g[:, 1:2], None, ALU.mult).then_inc(tables_done, 1)
            dve.wait_ge(tables_done, 1)

            def set_source(r, j):
                at_least(dve, gathered[j], 16 * r)
                hold(dve, counter)
                dve.tensor_copy(source_now[:, j:j + 1], source[:, ds(RING * r + j, 1)]).then_inc(source_set, 1)

            def low_part_xT(b, slot2):
                dve.wait_ge(xTH_done, b + 1)
                dve.tensor_tensor(xTL[:, slot2], ps_x[:, 0:P], xTH[:, slot2].bitcast(f32), ALU.subtract)\
                    .then_inc(xTL_done, 1)

            def low_part_hT(b, slot2):
                dve.wait_ge(hTH_done, b + 1)
                dve.tensor_tensor(hTL[:, slot2], ps_hT[slot2][:, :], hTH[:, slot2].bitcast(f32), ALU.subtract)\
                    .then_inc(hTL_done, 1)

            def evacuate_y(r, j):
                b = RING * r + j
                at_least(dve, scattered[j], 16 * r)
                hold(dve, counter)
                dve.tensor_copy(dest_now[:, j:j + 1], dest[:, ds(b, 1)]).then_inc(dest_set, 1)
                dve.wait_ge(y_psum, b + 1)
                dve.tensor_copy(y[:, j], ps_y[:, 0:D]).then_inc(y_done, 1)

            def shared_parts(s):
                dve.wait_ge(sT_done, s + 1)
                at_least(dve, sy_psum, s)
                dve.tensor_copy(sTH[:, :], sT[:, :]).then_inc(sTH_done, 1)
                dve.wait_ge(sTH_done, s + 1)
                dve.tensor_tensor(sTL[:, :], sT[:, :], sTH[:, :].bitcast(f32), ALU.subtract).then_inc(sTL_done, 1)

            def add_shared(s):
                dve.wait_ge(sy_psum, s + 1)
                dve.scalar_tensor_tensor(out=xres[:, ds(s * D, D)], in0=ps_sy[:, 0:D], scalar=tanh_g[:, 1:2],
                                         in1=xres[:, ds(s * D, D)], op0=ALU.mult, op1=ALU.add).then_inc(shared_done, 1)

            def dve_round(r, shared, first=False, last=False):
                for j in range(RING):
                    b = RING * r + j
                    if not (last and j + 2 >= RING):
                        low_part_xT(b + 2, j % 2)
                    if not (first and j == 0):
                        evacuate_y(*((r, j - 1) if j else (r - 1, RING - 1)))
                    low_part_hT(b, j % 2)
                    if not last:
                        set_source(r + 1, j)
                    if shared:
                        if j % 2 == 0:
                            shared_parts(SHARED_PER_ROUND * r + j // 2)
                        else:
                            add_shared(SHARED_PER_ROUND * r + j // 2)

            for j in range(RING):
                set_source(0, j)
            low_part_xT(0, 0)
            low_part_xT(1, 1)
            dve_round(0, True, first=True)
            with dve.Fori(1, SHARED_ROUNDS) as r:
                dve_round(r, True)
            with dve.Fori(SHARED_ROUNDS, ROUNDS - 1) as r:
                dve_round(r, False)
            dve_round(ROUNDS - 1, False, last=True)
            evacuate_y(ROUNDS - 1, RING - 1)

            dve.wait_ge(shared_done, TILES)

            def combine(qq, j):
                g = 2 * qq + j
                dve.wait_ge(y_loaded[j], 16 * K * (qq + 1))
                hold(dve, counter)
                for k in range(K):
                    for t in range(G):
                        cols = ds(g * GW + t * D, D)
                        dve.scalar_tensor_tensor(out=xres[:, cols], in0=y_in[:, j, k, t * D:(t + 1) * D],
                                                 scalar=gates[:, k, ds(g * G + t, 1)], in1=xres[:, cols],
                                                 op0=ALU.mult, op1=ALU.add).then_inc(out_done if k else half_done, 1)
                    if k == 0:
                        dve.wait_ge(half_done, G * (g + 1))
                        hold(dve, counter)

            with dve.Fori(0, GROUPS // 2) as qq:
                combine(qq, 0)
                combine(qq, 1)

        @block.tensor
        def _(pe):
            counter = pe_holds
            pe.wait_ge(consts_ready, 1)

            def matmul3(ps, aH, aL, bH, bL, start, stop):
                pe.matmul(ps, aH, bH, start=start, stop=False)
                pe.matmul(ps, aH, bL, start=False, stop=False)
                return pe.matmul(ps, aL, bH, start=False, stop=stop)

            def score(qq, j):
                g = 2 * qq + j
                pe.wait_ge(ctx_loaded[j], 16 * (qq + 1))
                at_least(pe, kT_done, g)
                for t in range(G):
                    last = pe.transpose(ps_k[:, t * P:(t + 1) * P], ctx_in[:, j, t * D:(t + 1) * D], ident[:, :])
                last.then_inc(kT_psum, 1)
                pe.wait_ge(kT_done, g + 1)
                at_least(pe, scores_done, g)
                for t in range(G):
                    k_t = kT[:, j, t * P:(t + 1) * P]
                    last = pe.matmul(ps_s[:, t * P:(t + 1) * P], k_t, k_t, start=True, stop=True)
                last.then_inc(s_psum, 1)

            def apply_scores(qq, j):
                g = 2 * qq + j
                pe.wait_ge(scores_done, g + 1)
                pe.wait_ge(q_done, g + 1)
                at_least(pe, x1_done, g)
                for t in range(G):
                    cols = slice(t * P, (t + 1) * P)
                    pe.matmul(ps_q[:, cols], scores[:, j, cols], q[:, j, cols], start=True, stop=False)
                    last = pe.matmul(ps_q[:, cols], ident[:, :], q[:, j, cols], start=False, stop=True)
                last.then_inc(attn_psum, 1)

            def transpose_n(qq, j):
                g = 2 * qq + j
                pe.wait_ge(n_done, G * (g + 1))
                at_least(pe, nTL_done, g)
                for t in range(G):
                    last = pe.transpose(ps_n[:, t * P:(t + 1) * P], n[:, j, t * D:(t + 1) * D], ident[:, :])
                last.then_inc(nT_psum, 1)

            run_phase_a(pe, (score, apply_scores, transpose_n))

            pe.wait_ge(small_in, 48)
            pe.wait_ge(kT_done, GROUPS)
            pe.transpose(ps_k[:, 0:E], gate_in[:, :], ident[0:E, 0:E]).then_inc(gate_psum, 1)
            pe.wait_ge(w_loaded, 16 * 2 * (1 + E // 2))
            for i in range(2 * (E + 1)):
                at_least(pe, wL_done, i - 1)
                for c in range(HC):
                    w_in = (w1_in, w2_in)[i % 2][:, (i // 2) * H + c * P:(i // 2) * H + (c + 1) * P]
                    last = pe.transpose(ps_w[i % 2][:, c * P:(c + 1) * P], w_in, ident[:, :])
                last.then_inc(w_psum, 1)
            pe.wait_ge(nTL_done, GROUPS)
            pe.wait_ge(route, 2)
            for t in range(TILES):
                cols = slice(t * P, (t + 1) * P)
                last = matmul3(ps_logit[:, t * E:(t + 1) * E], nTH[:, cols], nTL[:, cols], gTH[:, :], gTL[:, :],
                               start=True, stop=True)
            last.then_inc(logit_psum, 1)

            pe.wait_ge(picked_done, 1)
            cells = E * TILES
            by_expert = picked[:, :, :].rearrange("p t e -> p e t")
            pe.matmul(ps_before[:, 0:cells].rearrange("p (e t) -> p e t", e=E), before[:, :], by_expert, start=True, stop=True)
            pe.matmul(ps_total[:, 0:cells].rearrange("p (e t) -> p e t", e=E), ones[:, :], by_expert, start=True, stop=True)\
                .then_inc(prefix_psum, 1)
            for i in range(K * TILES):
                pe.wait_ge(onehot_done, 3 * (i + 1))
                pe.matmul(ps_inverse[:, 0:2 * BLOCKS], at_lane[:, i % 4], at_block[:, i % 4], start=(i == 0),
                          stop=(i == K * TILES - 1)).then_inc(onehot_used, 1)
            pe.wait_ge(tables_done, 1)

            def transpose_rows(r, j):
                b = RING * r + j
                pe.wait_ge(gathered[j], 16 * (r + 1))
                at_least(pe, xTL_done, b)
                pe.transpose(ps_x[:, 0:P], rows_in[:, j], ident[:, :]).then_inc(xT_psum, 1)

            def up(b, slot2):
                at = pe.value_load(weight_at[0:1, ds(b, 1)], min_val=0, max_val=(E - 1) * H)
                pe.wait_ge(xTL_done, b + 1)
                at_least(pe, h_done, b - 1)
                hold(pe, counter)
                matmul3(ps_up[slot2][:, :], xTH[:, slot2], xTL[:, slot2], w1H[:, ds(at, H)], w1L[:, ds(at, H)],
                        start=True, stop=True).then_inc(up_psum, 1)

            def transpose_h(b, slot2):
                pe.wait_ge(h_done, b + 1)
                at_least(pe, hTL_done, b - 1)
                for c in range(HC):
                    cols = slice(c * P, (c + 1) * P)
                    last = pe.transpose(ps_hT[slot2][:, cols], h[:, slot2, cols], ident[:, :])
                last.then_inc(hT_psum, 1)

            def down(b, slot2):
                at = pe.value_load(weight_at[0:1, ds(b, 1)], min_val=0, max_val=(E - 1) * H)
                pe.wait_ge(hTL_done, b + 1)
                at_least(pe, y_done, b)
                hold(pe, counter)
                for c in range(HC):
                    cols = slice(c * P, (c + 1) * P)
                    last = matmul3(ps_y[:, 0:D], hTH[:, slot2, cols], hTL[:, slot2, cols],
                                   w2H[:, ds(at + c * D, D)], w2L[:, ds(at + c * D, D)],
                                   start=(c == 0), stop=(c == HC - 1))
                last.then_inc(y_psum, 1)

            def shared_up(s):
                at_least(pe, sT_done, s)
                hold(pe, counter)
                for c in range(HC):
                    w = slice(E * H + c * P, E * H + (c + 1) * P)
                    last = matmul3(ps_sup[:, c * P:(c + 1) * P], w1H[:, w], w1L[:, w],
                                   nTH[:, ds(s * P, P)], nTL[:, ds(s * P, P)], start=True, stop=True)
                last.then_inc(sup_psum, 1)

            def shared_down(s):
                pe.wait_ge(sTL_done, s + 1)
                at_least(pe, shared_done, s)
                for c in range(HC):
                    cols = slice(c * P, (c + 1) * P)
                    w = slice(E * H + c * D, E * H + (c + 1) * D)
                    last = matmul3(ps_sy[:, 0:D], sTH[:, cols], sTL[:, cols], w2H[:, w], w2L[:, w],
                                   start=(c == 0), stop=(c == HC - 1))
                last.then_inc(sy_psum, 1)

            def pe_round(r, shared, first=False, last=False):
                for j in range(RING):
                    b = RING * r + j
                    if not (last and j + 2 >= RING):
                        transpose_rows(*((r, j + 2) if j + 2 < RING else (r + 1, j + 2 - RING)))
                    if not (last and j + 1 >= RING):
                        up(b + 1, (j + 1) % 2)
                    transpose_h(b, j % 2)
                    if shared and j % 2 == 0:
                        shared_up(SHARED_PER_ROUND * r + j // 2)
                    if not (first and j == 0):
                        down(b - 1, (j - 1) % 2)
                    if shared and j % 2 == 1:
                        shared_down(SHARED_PER_ROUND * r + j // 2)

            transpose_rows(0, 0)
            transpose_rows(0, 1)
            up(0, 0)
            pe_round(0, True, first=True)
            with pe.Fori(1, SHARED_ROUNDS) as r:
                pe_round(r, True)
            with pe.Fori(SHARED_ROUNDS, ROUNDS - 1) as r:
                pe_round(r, False)
            pe_round(ROUNDS - 1, False, last=True)
            down(BLOCKS - 1, (BLOCKS - 1) % 2)


_INS = ["x", "ctx_1024", "g_xattn", "g_ffn", "L0_ffn_shared_w1", "L0_ffn_shared_w2", "L0_ffn_experts_w1",
        "L0_ffn_experts_w2", "L0_ffn_gate_w"]


def kernel(**inputs):
    import numpy as np
    import concourse.bacc as bacc
    from concourse.bass_utils import run_bass_kernel_spmd

    nc = bacc.Bacc("TRN2", target_bir_lowering=False, num_devices=1)
    arrays, args = {}, []
    for name in _INS:
        a = np.ascontiguousarray(inputs[name])
        arrays[f"in_{name}"] = a
        args.append(nc.dram_tensor(f"in_{name}", a.shape, mybir.dt.from_np(a.dtype), kind="ExternalInput").ap())
    out = nc.dram_tensor("out", inputs["x"].shape, mybir.dt.float32, kind="ExternalOutput").ap()
    flamingo_gated_moe(nc, *args, out)
    r = run_bass_kernel_spmd(nc, [arrays], core_ids=[0])
    return r.results[0]["out"]
```

```python
import concourse.bass as bass
from concourse import mybir
from contextlib import ExitStack


def flamingo_gated_moe(nc, x, ctx, g_xattn, g_ffn, sw1, sw2, ew1, ew2, gate_w, out):
    f32 = mybir.dt.float32
    f32r = mybir.dt.float32r
    bf16 = mybir.dt.bfloat16
    i32 = mybir.dt.int32
    ALU = mybir.AluOpType
    ACT = mybir.ActivationFunctionType
    AX = mybir.AxisListType.X
    ds = bass.ds

    P = 128
    B, S, D = x.shape
    H = sw1.shape[0]
    E = gate_w.shape[0]
    K = 2
    T = B * S
    TILES = T // P
    HC = H // P
    G = 4
    GROUPS = TILES // G
    GW = G * D
    EPS = 1e-5
    LAGS = 3
    BLOCKS = (K * T + E * (P - 1)) // P
    RING = 8
    AHEAD = 6
    BLOCKS = -(-BLOCKS // RING) * RING
    ROUNDS = BLOCKS // RING
    P_SHIFT = P.bit_length() - 1
    FAR = -3.0e38
    PAIRS = 16

    x_rows = x.rearrange("b s d -> (b s) d").rearrange("(t p) d -> p t d", p=P)
    ctx_rows = ctx.rearrange("b s d -> (b s) d").rearrange("(t p) d -> p t d", p=P)
    out_rows = out.rearrange("b s d -> (b s) d").rearrange("(t p) d -> p t d", p=P)

    ew1_rows = ew1.rearrange("e (c p) d -> p (e c) d", p=P)
    ew2_rows = ew2.rearrange("e d h -> d e h")

    stack = ExitStack()
    with stack:
        def sb(name, shape, dt=f32):
            return stack.enter_context(nc.sbuf_tensor(name, shape, dt))

        def sem(name):
            return stack.enter_context(nc.semaphore(name))

        n_dram = nc.dram_tensor("n_rows", (T, D), f32, kind="Internal").ap()
        y_dram = nc.dram_tensor("y_rows", (K * T + BLOCKS * P, D), f32, kind="Internal").ap()
        n_rows = n_dram.rearrange("(t p) d -> p t d", p=P)
        y_by_choice = y_dram[0:K * T, :].rearrange("(k t p) d -> p k t d", p=P, k=K)

        xres = sb("xres", [P, TILES * D])
        nTH = sb("nTH", [D, T], f32r)
        nTL = sb("nTL", [D, T], f32r)
        w1H = sb("w1H", [D, (E + 1) * H], f32r)
        w1L = sb("w1L", [D, (E + 1) * H], f32r)
        w2 = sb("w2", [P, (E + 1) * HC, 2, D], f32r)
        w1_in = sb("w1_in", [P, (E + 1) * HC * D])
        w2_in = sb("w2_in", [D, (E + 1) * H])
        gate_in = sb("gate_in", [E, D])
        gT = sb("gT", [D, 2, E], f32r)
        ident = sb("ident", [P, P])
        mask = sb("mask", [P, P])
        ident4 = sb("ident4", [P, G, P], bf16)
        before = sb("before", [P, P], bf16)
        ones = sb("ones", [P, P], bf16)
        lane_row = sb("lane_row", [P, P], bf16)
        block_row = sb("block_row", [P, BLOCKS], bf16)
        block_start = sb("block_start", [1, BLOCKS])
        lane = sb("lane", [P, 1])
        pad_row = sb("pad_row", [P, BLOCKS])
        rev_expert = sb("rev_expert", [P, E])
        tanh_g = sb("tanh_g", [P, 2])
        ctx_in = sb("ctx_in", [P, 2, GW])
        stats = sb("stats", [P, 2, 2, G, 6])
        mv1 = sb("mv1", [P, 2, G, 2])
        rstd1 = sb("rstd1", [P, 2, G])
        mv2 = sb("mv2", [P, 2, G, 2])
        rstd2 = sb("rstd2", [P, 2, G])
        shift2 = sb("shift2", [P, 2, G])
        unused = sb("unused", [P, 1])
        minus_half = sb("minus_half", [P, G])
        neg_mean = sb("neg_mean", [P, 2, G])
        q = sb("q", [P, 2, GW])
        kT = sb("kT", [D, 2, GW])
        scores = sb("scores", [P, 2, GW])
        n = sb("n", [P, 2, GW])
        cells = E * TILES
        spare = [t[:, j, c * cells:(c + 1) * cells] for t in (kT, scores) for j in range(2) for c in range(GW // cells)]
        spare += [n[:, 1, c * cells:(c + 1) * cells] for c in range(GW // cells)]
        logit, work, work2, *pick = (v.rearrange("p (t e) -> p t e", e=E) for v in spare[:3 + K])
        total, upto, where, restart = (v.rearrange("p (e t) -> p e t", t=TILES) for v in spare[3 + K:7 + K])
        best = sb("best", [P, K, TILES])
        rank = sb("rank", [P, TILES])
        logit_high = sb("logit_high", [P, TILES, E])
        picked = sb("picked", [P, TILES, E], bf16)
        count_i = sb("count_i", [P, E], i32)
        padded = sb("padded", [P, E])
        upto_e = sb("upto_e", [P, E])
        ones_e = sb("ones_e", [P, E])
        start_e = sb("start_e", [P, E])
        passed = sb("passed", [1, BLOCKS, E])
        expert_f = sb("expert_f", [1, BLOCKS])
        weight_at = sb("weight_at", [1, BLOCKS], i32)
        slot = sb("slot", [P, K, TILES])
        slot_i = sb("slot_i", [P, K * TILES], i32)
        slot_lane_i = sb("slot_lane_i", [P, K * TILES], i32)
        slot_block_i = sb("slot_block_i", [P, K * TILES], i32)
        slot_lane = sb("slot_lane", [P, K * TILES])
        slot_block = sb("slot_block", [P, K * TILES])
        gate_e = sb("gate_e", [P, TILES])
        gate_d = sb("gate_d", [P, TILES])
        gates = sb("gates", [P, K, TILES])
        at_lane = w1_in[:, 0:K * TILES * P // 2].bitcast(bf16).rearrange("p (i d) -> p i d", d=P)
        at_block = w2_in[:, 0:K * TILES * BLOCKS].bitcast(bf16).rearrange("p (i d) -> p i d", d=2 * BLOCKS)
        inverse = sb("inverse", [P, 2 * BLOCKS])
        is_pad = sb("is_pad", [P, BLOCKS])
        dest_f = sb("dest_f", [P, BLOCKS])
        dest = sb("dest", [P, BLOCKS], i32)
        source = sb("source", [P, BLOCKS], i32)
        source_now = sb("source_now", [P, RING], i32)
        dest_now = sb("dest_now", [P, RING], i32)
        xTH = sb("xTH", [D, 2, P], f32r)
        xTL = sb("xTL", [D, 2, P], f32r)
        hTH = sb("hTH", [P, 2, HC * P], f32r)
        hTL = sb("hTL", [P, 2, HC * P], f32r)
        more_sTH = sb("more_sTH", [P, 2, G * P], f32r)
        more_sTL = sb("more_sTL", [P, 2, G * P], f32r)
        h = w2_in[:, 0:2 * H].rearrange("p (s h) -> p s h", s=2)
        rows_in = w2_in[:, 6 * H:6 * H + RING * D].rearrange("p (s d) -> p s d", s=RING)
        y = w2_in[:, 2 * H:2 * H + RING * D].rearrange("p (s d) -> p s d", s=RING)
        y_low = w2_in[:, 5 * H:5 * H + 2 * D].rearrange("p (s d) -> p s d", s=2)
        sT = [ctx_in[:, 0], ctx_in[:, 1], q[:, 0], q[:, 1]]
        shared_T = n[:, 0]
        sTH = [hTH[:, 0], hTH[:, 1], more_sTH[:, 0], more_sTH[:, 1]]
        sTL = [hTL[:, 0], hTL[:, 1], more_sTL[:, 0], more_sTL[:, 1]]
        y_in = w1_in[:, 0:2 * K * GW].rearrange("p (j k d) -> p j k d", j=2, k=K)

        scaled_y = w2_in[:, 6 * H:6 * H + 2 * GW].rearrange("p (s d) -> p s d", s=2)

        bank = [stack.enter_context(nc.psum_tensor(f"bank{i}", [P, 512], f32)) for i in range(8)]
        ps_k, ps_s, ps_q, ps_n, ps_logit = bank[0], bank[1], bank[2], bank[3], bank[4]
        ps_w = [bank[5], bank[6], bank[7]]
        ps_before, ps_total, ps_inverse = bank[2][:, 0:cells], bank[2][:, cells:2 * cells], bank[4]
        ps_sup, ps_sout, ps_srows = [bank[3], bank[5], bank[6], bank[7]], bank[0], bank[1]
        ps_x, ps_up = [bank[0], bank[7]], [bank[1], bank[2]]
        ps_hT, ps_y = [bank[3], bank[4]], [bank[5], bank[6]]

        pool_holds = sem("pool_holds")
        act_holds = sem("act_holds")
        dve_holds = sem("dve_holds")
        pe_holds = sem("pe_holds")
        consts_ready = sem("consts_ready")
        pool_steps = sem("pool_steps")
        small_in = sem("small_in")
        x_in = [sem(f"x_in{i}") for i in range(3)]
        ctx_loaded = [sem(f"ctx_loaded{j}") for j in range(2)]
        w_loaded = sem("w_loaded")
        tanh_done = sem("tanh_done")
        kT_psum = sem("kT_psum")
        kT_done = sem("kT_done")
        s_psum = sem("s_psum")
        scores_done = sem("scores_done")
        stats1_part = sem("stats1_part")
        stats1_done = sem("stats1_done")
        centred_done = sem("centred_done")
        q_done = sem("q_done")
        attn_psum = sem("attn_psum")
        x1_done = sem("x1_done")
        rstd1_part = sem("rstd1_part")
        rstd1_done = sem("rstd1_done")
        scale2_part = sem("scale2_part")
        scale2_done = sem("scale2_done")
        stats2_part = sem("stats2_part")
        stats2_done = sem("stats2_done")
        n_done = sem("n_done")
        n_stored = [sem(f"n_stored{j}") for j in range(2)]
        nT_psum = sem("nT_psum")
        nTH_done = sem("nTH_done")
        nTL_done = sem("nTL_done")
        gate_psum = sem("gate_psum")
        w_psum = sem("w_psum")
        wH_done = sem("wH_done")
        wL_done = sem("wL_done")
        logit_psum = sem("logit_psum")
        route = sem("route")
        gate_exp = sem("gate_exp")
        picked_done = sem("picked_done")
        prefix_psum = sem("prefix_psum")
        onehot_done = sem("onehot_done")
        inverse_psum = sem("inverse_psum")
        gate_gap_done = sem("gate_gap_done")
        tables_done = sem("tables_done")
        source_set = sem("source_set")
        dest_set = sem("dest_set")
        gathered = [sem(f"gathered{j}") for j in range(RING)]
        scattered = [sem(f"scattered{j}") for j in range(RING)]
        xT_psum = sem("xT_psum")
        xTH_done = sem("xTH_done")
        xTL_done = sem("xTL_done")
        up_psum = sem("up_psum")
        h_done = sem("h_done")
        hT_psum = sem("hT_psum")
        hTH_done = sem("hTH_done")
        hTL_done = sem("hTL_done")
        y_psum = sem("y_psum")
        y_done = sem("y_done")
        y_low_done = sem("y_low_done")
        sup_psum = sem("sup_psum")
        sT_done = sem("sT_done")
        sTH_done = sem("sTH_done")
        sTL_done = sem("sTL_done")
        sdown_done = sem("sdown_done")
        sout_done = sem("sout_done")
        srows_psum = sem("srows_psum")
        shared_done = sem("shared_done")
        scaled_done = sem("scaled_done")
        y_loaded = [sem(f"y_loaded{j}") for j in range(2)]
        half_done = sem("half_done")
        out_done = sem("out_done")
        stored = sem("stored")

        def at_least(eng, semaphore, value):
            if not (isinstance(value, int) and value <= 0):
                eng.wait_ge(semaphore, value)

        def hold(eng, counter):
            eng.sem_inc(counter, 1)

        def run_phase_a(eng, *stages):
            steps = GROUPS + LAGS
            head, tail = 4, GROUPS

            def step(half, j):
                for lag, stage in stages:
                    if isinstance(half, int):
                        g = 2 * half + j - lag
                        if 0 <= g < GROUPS:
                            stage(g // 2, g % 2)
                    else:
                        stage(half - (lag - j + 1) // 2, (j - lag) % 2)

            for i in range(head):
                step(i // 2, i % 2)
            with eng.Fori(head // 2, tail // 2) as half:
                step(half, 0)
                step(half, 1)
            for i in range(tail, steps):
                step(i // 2, i % 2)

        def run_shared(eng, up, down, rows_back=None, between=None):
            def group(s, first=False, last=False):
                for c in range(HC):
                    if c + 2 < HC:
                        up(s, c + 2)
                    elif not last:
                        up(s + 1, c + 2 - HC)
                    down(s, c)
                    if c == 0 and not first and rows_back:
                        rows_back(s - 1)

            up(0, 0)
            up(0, 1)
            group(0, first=True)
            group(1)
            if between:
                between()
            with eng.Fori(2, GROUPS - 1) as s:
                group(s)
            group(GROUPS - 1, last=True)
            if rows_back:
                rows_back(GROUPS - 1)

        block = stack.enter_context(nc.Block())

        @block.sync
        def _(sp):
            sp.dma_start(tanh_g[:, 0:1], g_xattn.rearrange("(a n) -> a n", a=1).to_broadcast([P, 1])).then_inc(small_in, 16)
            sp.dma_start(tanh_g[:, 1:2], g_ffn.rearrange("(a n) -> a n", a=1).to_broadcast([P, 1])).then_inc(small_in, 16)
            sp.dma_start(gate_in[:, :], gate_w).then_inc(small_in, 16)

            def load_ctx(qq, j):
                at_least(sp, kT_psum, 2 * qq + j - 1)
                sp.dma_start(ctx_in[:, j].rearrange("p (t d) -> p t d", d=D),
                             ctx_rows[:, ds((2 * qq + j) * G, G), :]).then_inc(ctx_loaded[j], 16)

            def store_n(qq, j):
                g = 2 * qq + j
                sp.wait_ge(n_done, G * (g + 1))
                sp.dma_start(n_rows[:, ds(g * G, G), :],
                             n[:, j].rearrange("p (t d) -> p t d", d=D)).then_inc(n_stored[j], 16)

            load_ctx(0, 0)
            for part, (a, b) in enumerate(((0, G), (G, 2 * G), (2 * G, TILES))):
                sp.dma_start(xres[:, a * D:b * D].rearrange("p (t d) -> p t d", d=D),
                             x_rows[:, a:b, :]).then_inc(x_in[part], 16)
                if part == 0:
                    load_ctx(0, 1)

            sp.dma_start(w1_in[:, E * H:].rearrange("p (c d) -> p c d", d=D),
                         sw1.rearrange("(c p) d -> p c d", p=P)).then_inc(w_loaded, 16)
            sp.dma_start(w2_in[:, E * H:], sw2).then_inc(w_loaded, 16)

            def step(half, j):
                if not (isinstance(half, int) and 2 * half + j >= GROUPS):
                    load_ctx(half, j)
                g = 2 * half + j - LAGS
                if not isinstance(half, int):
                    store_n(half - (2 if j == 0 else 1), 1 - j)
                elif g >= 0:
                    store_n(g // 2, g % 2)

            def load_experts(first):
                count = E // 2
                sp.dma_start(w1_in[:, first * H:(first + count) * H].rearrange("p (a d) -> p a d", d=D),
                             ew1_rows[:, first * HC:(first + count) * HC, :]).then_inc(w_loaded, 16)
                sp.dma_start(w2_in[:, first * H:(first + count) * H].rearrange("p (e h) -> p e h", h=H),
                             ew2_rows[:, first:first + count, :]).then_inc(w_loaded, 16)

            step(1, 0)
            step(1, 1)
            load_experts(0)
            with sp.Fori(2, GROUPS // 2) as half:
                step(half, 0)
                step(half, 1)
            load_experts(E // 2)
            for i in range(GROUPS, GROUPS + LAGS):
                step(i // 2, i % 2)

            for j in range(RING):
                sp.wait_ge(scattered[j], 16 * ROUNDS)

            def load_y(qq, j):
                at_least(sp, out_done, 2 * qq + j - 1)
                for k in range(K):
                    sp.dma_start(y_in[:, j, k].rearrange("p (t d) -> p t d", d=D),
                                 y_by_choice[:, k, ds((2 * qq + j) * G, G), :]).then_inc(y_loaded[j], 16)

            def store_out(qq, j):
                g = 2 * qq + j
                sp.wait_ge(out_done, g + 1)
                sp.dma_start(out_rows[:, ds(g * G, G), :],
                             xres[:, ds(g * GW, GW)].rearrange("p (t d) -> p t d", d=D)).then_inc(stored, 16)

            load_y(0, 0)
            load_y(0, 1)
            with sp.Fori(1, GROUPS // 2) as qq:
                for j in range(2):
                    load_y(qq, j)
                    store_out(qq - 1, j)
            store_out(GROUPS // 2 - 1, 0)
            store_out(GROUPS // 2 - 1, 1)
            sp.wait_ge(stored, 16 * GROUPS)

        @block.gpsimd
        def _(pool):
            counter = pool_holds
            step = [0]

            def chained(instruction):
                step[0] += 1
                instruction.then_inc(pool_steps, 1)
                pool.wait_ge(pool_steps, step[0])

            chained(pool.memset(ident[:, :], 0.0))
            chained(pool.affine_select(out=ident[:, :], in_=ident[:, :], compare_op=ALU.not_equal, fill=1.0,
                                       base=0, pattern=[[-1, P]], channel_multiplier=1))
            chained(pool.memset(ident4[:, :, :], 0.0))
            chained(pool.affine_select(out=ident4[:, :, :], in_=ident4[:, :, :], compare_op=ALU.not_equal, fill=1.0,
                                       base=0, pattern=[[0, G], [-1, P]], channel_multiplier=1))
            chained(pool.memset(mask[:, :], 1.0))
            chained(pool.affine_select(out=mask[:, :], in_=mask[:, :], compare_op=ALU.is_ge, fill=0.0,
                                       base=0, pattern=[[1, P]], channel_multiplier=-1))
            chained(pool.affine_select(out=mask[:, S:P], in_=mask[:, S:P], compare_op=ALU.is_ge, fill=0.0,
                                       base=-S, pattern=[[0, P - S]], channel_multiplier=1))
            chained(pool.memset(before[:, :], 1.0))
            chained(pool.affine_select(out=before[:, :], in_=before[:, :], compare_op=ALU.is_gt, fill=0.0,
                                       base=0, pattern=[[1, P]], channel_multiplier=-1))
            chained(pool.memset(ones[:, :], 1.0))
            chained(pool.memset(ones_e[:, :], 1.0))
            chained(pool.memset(minus_half[:, :], -0.5))
            chained(pool.iota(lane_row[:, :], pattern=[[1, P]], base=0, channel_multiplier=0,
                              allow_small_or_imprecise_dtypes=True))
            chained(pool.iota(block_row[:, :], pattern=[[1, BLOCKS]], base=0, channel_multiplier=0,
                              allow_small_or_imprecise_dtypes=True))
            chained(pool.iota(block_start[:, :], pattern=[[P, BLOCKS]], base=0, channel_multiplier=0,
                              allow_small_or_imprecise_dtypes=True))
            chained(pool.iota(lane[:, :], pattern=[[0, 1]], base=0, channel_multiplier=1,
                              allow_small_or_imprecise_dtypes=True))
            chained(pool.iota(pad_row[:, :], pattern=[[P, BLOCKS]], base=K * T + P, channel_multiplier=1,
                              allow_small_or_imprecise_dtypes=True))
            chained(pool.iota(rev_expert[:, :], pattern=[[-1, E]], base=E, channel_multiplier=0,
                              allow_small_or_imprecise_dtypes=True))
            pool.memset(unused[:, :], 0.0).then_inc(consts_ready, 1)

            def centre_and_scale(qq, j):
                g = 2 * qq + j
                xg = xres[:, ds(g * GW, GW)].rearrange("p (t d) -> p t d", d=D)
                at_least(pool, attn_psum, g - 1)
                pool.wait_ge(stats1_done, g + 1)
                hold(pool, counter)
                pool.tensor_scalar(rstd1[:, j], mv1[:, j, :, 1], EPS, None, ALU.add).then_inc(rstd1_part, 1)
                pool.wait_ge(rstd1_part, g + 1)
                pool.tensor_tensor(rstd1[:, j], rstd1[:, j], minus_half[:, :], ALU.pow).then_inc(rstd1_done, 1)
                pool.tensor_tensor(q[:, j].rearrange("p (t d) -> p t d", d=D), xg,
                                   mv1[:, j, :, 0:1].to_broadcast([P, G, D]), ALU.subtract).then_inc(centred_done, 1)
                pool.wait_ge(rstd1_done, g + 1)
                hold(pool, counter)
                pool.wait_ge(centred_done, g + 1)
                pool.tensor_tensor(q[:, j].rearrange("p (t d) -> p t d", d=D),
                                   q[:, j].rearrange("p (t d) -> p t d", d=D),
                                   rstd1[:, j].unsqueeze(2).to_broadcast([P, G, D]), ALU.mult).then_inc(q_done, 1)

            def scale_and_shift(qq, j):
                g = 2 * qq + j
                at_least(pool, n_done, G * (g - 1))
                hold(pool, counter)
                pool.wait_ge(stats2_done, g + 1)
                hold(pool, counter)
                pool.tensor_scalar(rstd2[:, j], mv2[:, j, :, 1], EPS, None, ALU.add).then_inc(scale2_part, 1)
                pool.tensor_scalar(neg_mean[:, j], mv2[:, j, :, 0], -1.0, None, ALU.mult).then_inc(scale2_part, 1)
                pool.wait_ge(scale2_part, 3 * g + 2)
                pool.tensor_tensor(rstd2[:, j], rstd2[:, j], minus_half[:, :], ALU.pow).then_inc(scale2_part, 1)
                pool.wait_ge(scale2_part, 3 * g + 3)
                pool.tensor_tensor(shift2[:, j], neg_mean[:, j], rstd2[:, j], ALU.mult).then_inc(scale2_done, 1)

            run_phase_a(pool, (0, centre_and_scale), (2, scale_and_shift))

            def shared_low_part(s, c):
                i = HC * s + c
                at_least(pool, sdown_done, i - HC + 1)
                hold(pool, counter)
                pool.wait_ge(sTH_done, i + 1)
                pool.tensor_tensor(sTL[c], sT[c], sTH[c].bitcast(f32), ALU.subtract)\
                    .then_inc(sTL_done, 1)

            run_shared(pool, shared_low_part, lambda s, c: None)

            def gather(r, j):
                b = RING * r + j
                pool.wait_ge(source_set, b + 1)
                hold(pool, counter)
                if not (isinstance(b, int) and b < RING):
                    pool.wait_ge(xT_psum, b - RING + 1)
                    hold(pool, counter)
                pool.indirect_dma_start(out=rows_in[:, j], out_offset=None, in_=n_dram[:, :],
                                        in_offset=bass.IndirectOffsetOnAxis(ap=source_now[:, j:j + 1], axis=0))\
                    .then_inc(gathered[j], 16)

            def scatter(r, j):
                b = RING * r + j
                pool.wait_ge(y_done, b + 1)
                hold(pool, counter)
                pool.indirect_dma_start(out=y_dram[:, :],
                                        out_offset=bass.IndirectOffsetOnAxis(ap=dest_now[:, j:j + 1], axis=0),
                                        in_=y[:, j], in_offset=None).then_inc(scattered[j], 16)

            pool.wait_ge(inverse_psum, 1)
            for j in range(2):
                pool.wait_ge(n_stored[j], 16 * (GROUPS // 2))
            for j in range(RING):
                gather(0, j)
            with pool.Fori(1, ROUNDS) as r:
                for j in range(RING):
                    gather(r, j)
                    scatter(r - 1, j)
            for j in range(RING):
                scatter(ROUNDS - 1, j)

            def add_second(half, j):
                g = 2 * half + j
                pool.wait_ge(scaled_done, G * (g + 1))
                hold(pool, counter)
                pool.wait_ge(half_done, G * (g + 1))
                hold(pool, counter)
                cols = ds(g * GW, GW)
                pool.tensor_tensor(xres[:, cols], xres[:, cols], scaled_y[:, j], ALU.add).then_inc(out_done, 1)

            with pool.Fori(0, GROUPS // 2) as half:
                add_second(half, 0)
                add_second(half, 1)

        @block.scalar
        def _(act):
            counter = act_holds
            act.preload_act_table(ACT.Silu)
            act.wait_ge(small_in, 48)
            act.activation(tanh_g[:, :], tanh_g[:, :], ACT.Tanh).then_inc(tanh_done, 1)

            def evacuate_kT(qq, j):
                g = 2 * qq + j
                at_least(act, s_psum, g - 1)
                act.wait_ge(kT_psum, g + 1)
                act.activation(kT[:, j], ps_k[:, :], ACT.Copy).then_inc(kT_done, 1)

            def normalise(qq, j):
                g = 2 * qq + j
                at_least(act, n_stored[j], 16 * qq)
                at_least(act, nT_psum, g - 1)
                act.wait_ge(scale2_done, g + 1)
                hold(act, counter)
                for t in range(G):
                    act.activation(n[:, j, t * D:(t + 1) * D], xres[:, ds(g * GW + t * D, D)], ACT.Identity,
                                   bias=shift2[:, j, t:t + 1], scale=rstd2[:, j, t:t + 1]).then_inc(n_done, 1)

            def high_part_nT(qq, j):
                g = 2 * qq + j
                act.wait_ge(nT_psum, g + 1)
                hold(act, counter)
                act.activation(nTH[:, ds(g * GW, GW)], ps_n[:, :], ACT.Copy).then_inc(nTH_done, 1)

            run_phase_a(act, (0, evacuate_kT), (3, high_part_nT), (2, normalise))

            for i in range(2 * (E + 1)):
                act.wait_ge(w_psum, i + 1)
                e = i // 2
                ps = ps_w[i % 3][:, :]
                if i % 2 == 0:
                    act.activation(w1H[:, e * H:(e + 1) * H], ps, ACT.Copy).then_inc(wH_done, 1)
                else:
                    act.activation(w2[:, e * HC:(e + 1) * HC, 0, :], ps.rearrange("p (c d) -> p c d", d=D),
                                   ACT.Copy).then_inc(wH_done, 1)

            def shared_silu(s, c):
                i = HC * s + c
                act.wait_ge(sup_psum, i + 1)
                at_least(act, sTL_done, i - HC + 1)
                act.activation(sT[c], ps_sup[c][:, :], ACT.Silu).then_inc(sT_done, 1)
                at_least(act, sdown_done, i - HC + 1)
                act.wait_ge(sT_done, i + 1)
                act.activation(sTH[c], sT[c], ACT.Copy).then_inc(sTH_done, 1)

            def shared_scaled(s):
                act.wait_ge(sdown_done, HC * (s + 1))
                at_least(act, srows_psum, s)
                act.activation(shared_T, ps_sout[:, :], ACT.Copy, scale=tanh_g[:, 1:2]).then_inc(sout_done, 1)

            def down(s, c):
                if c == HC - 1:
                    shared_scaled(s)

            for j in range(2):
                act.wait_ge(n_stored[j], 16 * (GROUPS // 2))
            run_shared(act, shared_silu, down)

            act.wait_ge(gate_gap_done, 1)
            act.activation(gate_e[:, :], gate_d[:, :], ACT.Exp).then_inc(gate_exp, 1)
            act.preload_act_table(ACT.Silu)

            def high_part_xT(b, slot2):
                act.wait_ge(xT_psum, b + 1)
                at_least(act, up_psum, b - 1)
                act.activation(xTH[:, slot2], ps_x[slot2][:, 0:P], ACT.Copy).then_inc(xTH_done, 1)

            def silu(b, slot2):
                act.wait_ge(up_psum, b + 1)
                at_least(act, hT_psum, b - 1)
                act.activation(h[:, slot2], ps_up[slot2][:, :], ACT.Silu).then_inc(h_done, 1)

            def high_part_hT(b, slot2):
                act.wait_ge(hT_psum, b + 1)
                at_least(act, y_psum, b - 1)
                act.activation(hTH[:, slot2], ps_hT[slot2][:, :], ACT.Copy).then_inc(hTH_done, 1)

            def evacuate_low_y(b, slot2):
                act.wait_ge(y_psum, b + 1)
                at_least(act, y_done, b - 1)
                act.activation(y_low[:, slot2], ps_y[slot2][:, D:2 * D], ACT.Copy).then_inc(y_low_done, 1)

            def act_round(r, first=False, last=False):
                for j in range(RING):
                    b = RING * r + j
                    if not (last and j + 2 >= RING):
                        high_part_xT(b + 2, j % 2)
                    if not (last and j + 1 >= RING):
                        silu(b + 1, (j + 1) % 2)
                    high_part_hT(b, j % 2)
                    if not (first and j == 0):
                        evacuate_low_y(b - 1, (j - 1) % 2)

            high_part_xT(0, 0)
            high_part_xT(1, 1)
            silu(0, 0)
            act_round(0, first=True)
            with act.Fori(1, ROUNDS - 1) as r:
                act_round(r)
            act_round(ROUNDS - 1, last=True)
            evacuate_low_y(BLOCKS - 1, (BLOCKS - 1) % 2)

            def scale_second(half, j):
                g = 2 * half + j
                act.wait_ge(y_loaded[j], 16 * K * (half + 1))
                hold(act, counter)
                if not (isinstance(half, int) and half == 0):
                    act.wait_ge(out_done, g - 1)
                    hold(act, counter)
                for t in range(G):
                    act.activation(scaled_y[:, j, t * D:(t + 1) * D], y_in[:, j, 1, t * D:(t + 1) * D], ACT.Copy,
                                   scale=gates[:, 1, ds(g * G + t, 1)]).then_inc(scaled_done, 1)

            scale_second(0, 0)
            scale_second(0, 1)
            with act.Fori(1, GROUPS // 2) as half:
                scale_second(half, 0)
                scale_second(half, 1)

        @block.vector
        def _(dve):
            counter = dve_holds
            step = [0]

            def chained(instruction):
                step[0] += 1
                instruction.then_inc(route, 1)
                dve.wait_ge(route, step[0])

            dve.wait_ge(consts_ready, 1)
            dve.wait_ge(tanh_done, 1)

            def mean_variance(src, mv, which, j, part, before_parts):
                for t in range(G):
                    dve.bn_stats(stats[:, which, j, t, :], src(t)).then_inc(part, 1)
                dve.wait_ge(part, before_parts + G)
                hold(dve, counter)
                for t in range(G):
                    last = dve.bn_aggr(mv[:, j, t, :], stats[:, which, j, t, :])
                return last

            def statistics(qq, j):
                g = 2 * qq + j
                if isinstance(qq, int):
                    dve.wait_ge(x_in[min(g, 2)], 16)
                else:
                    dve.wait_ge(x_in[2], 16)
                at_least(dve, q_done, g - 1)
                hold(dve, counter)
                mean_variance(lambda t: xres[:, ds(g * GW + t * D, D)], mv1, 0, j, stats1_part, G * g)\
                    .then_inc(stats1_done, 1)

            def mask_scores(qq, j):
                g = 2 * qq + j
                at_least(dve, attn_psum, g - 1)
                dve.wait_ge(s_psum, g + 1)
                dve.tensor_tensor(scores[:, j].rearrange("p (t d) -> p t d", d=P),
                                  ps_s[:, :].rearrange("p (t d) -> p t d", d=P),
                                  mask[:, :].unsqueeze(1).to_broadcast([P, G, P]), ALU.mult).then_inc(scores_done, 1)

            def residual(qq, j):
                g = 2 * qq + j
                dve.wait_ge(attn_psum, g + 1)
                dve.scalar_tensor_tensor(out=xres[:, ds(g * GW, GW)], in0=ps_q[:, :], scalar=tanh_g[:, 0:1],
                                         in1=xres[:, ds(g * GW, GW)], op0=ALU.mult, op1=ALU.add).then_inc(x1_done, 1)
                dve.wait_ge(x1_done, g + 1)
                hold(dve, counter)
                at_least(dve, n_done, G * (g - 1))
                hold(dve, counter)
                mean_variance(lambda t: xres[:, ds(g * GW + t * D, D)], mv2, 1, j, stats2_part, G * g)\
                    .then_inc(stats2_done, 1)

            def low_part_nT(qq, j):
                g = 2 * qq + j
                dve.wait_ge(nTH_done, g + 1)
                dve.tensor_tensor(nTL[:, ds(g * GW, GW)], ps_n[:, :], nTH[:, ds(g * GW, GW)].bitcast(f32),
                                  ALU.subtract).then_inc(nTL_done, 1)

            run_phase_a(dve, (0, statistics), (2, residual), (1, mask_scores), (3, low_part_nT))

            dve.wait_ge(gate_psum, 1)
            chained(dve.tensor_copy(gT[:, 0], ps_k[:, 0:E]))
            chained(dve.tensor_tensor(gT[:, 1], ps_k[:, 0:E], gT[:, 0].bitcast(f32), ALU.subtract))

            for i in range(2 * (E + 1)):
                dve.wait_ge(wH_done, i + 1)
                e = i // 2
                ps = ps_w[i % 3][:, :]
                if i % 2 == 0:
                    cols = slice(e * H, (e + 1) * H)
                    dve.tensor_tensor(w1L[:, cols], ps, w1H[:, cols].bitcast(f32), ALU.subtract).then_inc(wL_done, 1)
                else:
                    rows = slice(e * HC, (e + 1) * HC)
                    dve.tensor_tensor(w2[:, rows, 1, :], ps.rearrange("p (c d) -> p c d", d=D),
                                      w2[:, rows, 0, :].bitcast(f32), ALU.subtract).then_inc(wL_done, 1)

            def add_shared(s):
                dve.wait_ge(srows_psum, s + 1)
                cols = slice(s * GW, (s + 1) * GW)
                dve.tensor_tensor(xres[:, cols], ps_srows[:, :], xres[:, cols], ALU.add).then_inc(shared_done, 1)

            dve.wait_ge(logit_psum, 1)
            dve.wait_ge(n_stored[1], 16 * (GROUPS // 2))
            chained(dve.memset(restart[:, :, :], 1.0))
            chained(dve.memset(restart[:, :, 0:1], 0.0))
            logit_parts = ps_logit[:, :].rearrange("p (t k e) -> p t k e", k=2, e=E)
            chained(dve.tensor_copy(logit_high[:, :, :], logit_parts[:, :, 0, :]))
            chained(dve.tensor_tensor(logit[:, :, :], logit_parts[:, :, 1, :], logit_high[:, :, :], ALU.add))
            rev = rev_expert[:, :].unsqueeze(1).to_broadcast([P, TILES, E])
            left = logit
            for k in range(K):
                top = best[:, k].unsqueeze(2)
                chained(dve.tensor_reduce(best[:, k], left[:, :, :], AX, ALU.max))
                chained(dve.tensor_tensor(work[:, :, :], left[:, :, :], top.to_broadcast([P, TILES, E]), ALU.is_equal))
                chained(dve.tensor_tensor(work[:, :, :], work[:, :, :], rev, ALU.mult))
                chained(dve.tensor_reduce(rank[:, :], work[:, :, :], AX, ALU.max))
                chained(dve.tensor_tensor(pick[k][:, :, :], rank[:, :].unsqueeze(2).to_broadcast([P, TILES, E]), rev,
                                          ALU.is_equal))
                if k == 0:
                    chained(dve.scalar_tensor_tensor(out=work2[:, :, :], in0=pick[0][:, :, :], scalar=FAR,
                                                     in1=logit[:, :, :], op0=ALU.mult, op1=ALU.add))
                    left = work2
            dve.tensor_tensor(gate_d[:, :], best[:, 1], best[:, 0], ALU.subtract).then_inc(gate_gap_done, 1)
            dve.tensor_tensor(picked[:, :, :], pick[0][:, :, :], pick[1][:, :, :], ALU.add).then_inc(picked_done, 1)
            add_shared(0)
            dve.wait_ge(prefix_psum, 1)
            by_expert = "p (e t) -> p e t"
            chained(dve.tensor_copy(total[:, :, :], ps_total.rearrange(by_expert, t=TILES)))
            chained(dve.tensor_tensor_scan(upto[:, :, :].rearrange("p e t -> p (e t)"), restart[:, :, :].rearrange("p e t -> p (e t)"),
                                           total[:, :, :].rearrange("p e t -> p (e t)"), 0.0, ALU.mult, ALU.add))
            chained(dve.tensor_scalar(count_i[:, :], upto[:, :, TILES - 1], float(P - 1), None, ALU.add))
            chained(dve.tensor_scalar(count_i[:, :], count_i[:, :], P_SHIFT, P_SHIFT, ALU.logical_shift_right,
                                      ALU.logical_shift_left))
            chained(dve.tensor_copy(padded[:, :], count_i[:, :]))
            chained(dve.tensor_tensor_scan(upto_e[:, :], ones_e[:, :], padded[:, :], 0.0, ALU.mult, ALU.add))
            chained(dve.tensor_tensor(start_e[:, :], upto_e[:, :], padded[:, :], ALU.subtract))
            chained(dve.tensor_tensor(passed[:, :, :], upto_e[0:1, :].unsqueeze(1).to_broadcast([1, BLOCKS, E]),
                                      block_start[:, :].unsqueeze(2).to_broadcast([1, BLOCKS, E]), ALU.is_le))
            chained(dve.tensor_reduce(expert_f[:, :], passed[:, :, :], AX, ALU.add))
            chained(dve.tensor_scalar(weight_at[:, :], expert_f[:, :], float(E - 1), float(H), ALU.min, ALU.mult))
            add_shared(1)
            chained(dve.tensor_tensor(where[:, :, :], upto[:, :, :], total[:, :, :], ALU.subtract))
            chained(dve.tensor_tensor(where[:, :, :], where[:, :, :],
                                      start_e[:, :].unsqueeze(2).to_broadcast([P, E, TILES]), ALU.add))
            chained(dve.tensor_tensor(where[:, :, :], where[:, :, :],
                                      ps_before.rearrange(by_expert, t=TILES), ALU.add))
            for k in range(K):
                chained(dve.tensor_tensor(work[:, :, :], where[:, :, :].rearrange("p e t -> p t e"), pick[k][:, :, :],
                                          ALU.mult))
                chained(dve.tensor_reduce(slot[:, k], work[:, :, :], AX, ALU.add))
            chained(dve.tensor_copy(slot_i[:, :], slot[:, :, :].rearrange("p k t -> p (k t)")))
            chained(dve.tensor_scalar(slot_lane_i[:, :], slot_i[:, :], P - 1, None, ALU.bitwise_and))
            chained(dve.tensor_scalar(slot_block_i[:, :], slot_i[:, :], P_SHIFT, None, ALU.logical_shift_right))
            chained(dve.tensor_copy(slot_lane[:, :], slot_lane_i[:, :]))
            chained(dve.tensor_copy(slot_block[:, :], slot_block_i[:, :]))
            add_shared(2)
            for i in range(K * TILES):
                dve.tensor_scalar(at_lane[:, i], lane_row[:, :], slot_lane[:, i:i + 1], None, ALU.is_equal)
                dve.tensor_scalar(at_block[:, i, 0:BLOCKS], block_row[:, :], slot_block[:, i:i + 1], float(i + 1),
                                  ALU.is_equal, ALU.mult)
                last = dve.tensor_scalar(at_block[:, i, BLOCKS:], block_row[:, :], slot_block[:, i:i + 1],
                                         lane[:, 0:1], ALU.is_equal, ALU.mult)
                if (i + 1) % PAIRS == 0:
                    last.then_inc(onehot_done, 1)
                    add_shared(3 + i // PAIRS)
            add_shared(GROUPS - 1)
            dve.wait_ge(inverse_psum, 1)
            chained(dve.tensor_copy(inverse[:, :], ps_inverse[:, 0:2 * BLOCKS]))
            chained(dve.scalar_tensor_tensor(out=dest_f[:, :], in0=inverse[:, 0:BLOCKS], scalar=float(P),
                                             in1=inverse[:, BLOCKS:], op0=ALU.mult, op1=ALU.add))
            chained(dve.scalar_tensor_tensor(out=is_pad[:, :], in0=inverse[:, 0:BLOCKS], scalar=0.0,
                                             in1=pad_row[:, :], op0=ALU.is_equal, op1=ALU.mult))
            chained(dve.scalar_tensor_tensor(out=dest[:, :], in0=dest_f[:, :], scalar=-float(P), in1=is_pad[:, :],
                                             op0=ALU.add, op1=ALU.add))
            chained(dve.tensor_scalar(source[:, :], dest[:, :], T - 1, None, ALU.bitwise_and))
            dve.wait_ge(gate_exp, 1)
            chained(dve.tensor_scalar(gate_d[:, :], gate_e[:, :], 1.0, None, ALU.add))
            chained(dve.reciprocal(gates[:, 0], gate_d[:, :]))
            chained(dve.tensor_tensor(gates[:, 1], gates[:, 0], gate_e[:, :], ALU.mult))
            dve.tensor_scalar(gates[:, :, :], gates[:, :, :], tanh_g[:, 1:2], None, ALU.mult).then_inc(tables_done, 1)
            dve.wait_ge(tables_done, 1)

            def set_source(r, j):
                at_least(dve, gathered[j], 16 * r)
                hold(dve, counter)
                dve.tensor_copy(source_now[:, j:j + 1], source[:, ds(RING * r + j, 1)]).then_inc(source_set, 1)

            def low_part_xT(b, slot2):
                dve.wait_ge(xTH_done, b + 1)
                dve.tensor_tensor(xTL[:, slot2], ps_x[slot2][:, 0:P], xTH[:, slot2].bitcast(f32), ALU.subtract)\
                    .then_inc(xTL_done, 1)

            def low_part_hT(b, slot2):
                dve.wait_ge(hTH_done, b + 1)
                dve.tensor_tensor(hTL[:, slot2], ps_hT[slot2][:, :], hTH[:, slot2].bitcast(f32), ALU.subtract)\
                    .then_inc(hTL_done, 1)

            def evacuate_y(r, j):
                b = RING * r + j
                at_least(dve, scattered[j], 16 * r)
                hold(dve, counter)
                dve.tensor_copy(dest_now[:, j:j + 1], dest[:, ds(b, 1)]).then_inc(dest_set, 1)
                dve.wait_ge(y_low_done, b + 1)
                dve.tensor_tensor(y[:, j], ps_y[j % 2][:, 0:D], y_low[:, j % 2], ALU.add).then_inc(y_done, 1)

            def dve_round(r, first=False, last=False):
                for j in range(RING):
                    b = RING * r + j
                    if not (last and j + 2 >= RING):
                        low_part_xT(b + 2, j % 2)
                    low_part_hT(b, j % 2)
                    if j + AHEAD < RING:
                        if first:
                            set_source(0, j + AHEAD)
                        else:
                            set_source(r, j + AHEAD)
                    elif not last:
                        set_source(r + 1, j + AHEAD - RING)
                    if not (first and j == 0):
                        evacuate_y(*((r, j - 1) if j else (r - 1, RING - 1)))

            for j in range(AHEAD):
                set_source(0, j)
            low_part_xT(0, 0)
            low_part_xT(1, 1)
            dve_round(0, first=True)
            with dve.Fori(1, ROUNDS - 1) as r:
                dve_round(r)
            dve_round(ROUNDS - 1, last=True)
            evacuate_y(ROUNDS - 1, RING - 1)

            dve.wait_ge(shared_done, GROUPS)

            def combine(qq, j):
                g = 2 * qq + j
                dve.wait_ge(y_loaded[j], 16 * K * (qq + 1))
                hold(dve, counter)
                for t in range(G):
                    cols = ds(g * GW + t * D, D)
                    dve.scalar_tensor_tensor(out=xres[:, cols], in0=y_in[:, j, 0, t * D:(t + 1) * D],
                                             scalar=gates[:, 0, ds(g * G + t, 1)], in1=xres[:, cols],
                                             op0=ALU.mult, op1=ALU.add).then_inc(half_done, 1)

            with dve.Fori(0, GROUPS // 2) as qq:
                combine(qq, 0)
                combine(qq, 1)

        @block.tensor
        def _(pe):
            counter = pe_holds
            pe.wait_ge(consts_ready, 1)

            def matmul3(ps, aH, aL, bH, bL, start, stop):
                pe.matmul(ps, aH, bH, start=start, stop=False)
                pe.matmul(ps, aH, bL, start=False, stop=False)
                return pe.matmul(ps, aL, bH, start=False, stop=stop)

            def transpose_k(qq, j):
                g = 2 * qq + j
                pe.wait_ge(ctx_loaded[j], 16 * (qq + 1))
                at_least(pe, kT_done, g)
                for t in range(G):
                    last = pe.transpose(ps_k[:, t * P:(t + 1) * P], ctx_in[:, j, t * D:(t + 1) * D], ident[:, :])
                last.then_inc(kT_psum, 1)

            def score(qq, j):
                g = 2 * qq + j
                pe.wait_ge(kT_done, g + 1)
                at_least(pe, scores_done, g)
                pe.matmul(ps_s[:, :], ident4[:, 0], ident4[:, :, :].rearrange("p t d -> p (t d)"), start=True, stop=False,
                          skip_group_check=True)
                for t in range(G):
                    k_t = kT[:, j, t * P:(t + 1) * P]
                    last = pe.matmul(ps_s[:, t * P:(t + 1) * P], k_t, k_t, start=False, stop=(t == G - 1),
                                     skip_group_check=True)
                last.then_inc(s_psum, 1)

            def apply_scores(qq, j):
                g = 2 * qq + j
                pe.wait_ge(scores_done, g + 1)
                pe.wait_ge(q_done, g + 1)
                at_least(pe, x1_done, g)
                for t in range(G):
                    cols = slice(t * P, (t + 1) * P)
                    last = pe.matmul(ps_q[:, cols], scores[:, j, cols], q[:, j, cols], start=True, stop=True)
                last.then_inc(attn_psum, 1)

            def transpose_n(qq, j):
                g = 2 * qq + j
                pe.wait_ge(n_done, G * (g + 1))
                at_least(pe, nTL_done, g)
                for t in range(G):
                    last = pe.transpose(ps_n[:, t * P:(t + 1) * P], n[:, j, t * D:(t + 1) * D], ident[:, :])
                last.then_inc(nT_psum, 1)

            run_phase_a(pe, (2, apply_scores), (1, score), (0, transpose_k), (3, transpose_n))

            pe.wait_ge(small_in, 48)
            pe.wait_ge(kT_done, GROUPS)
            pe.transpose(ps_k[:, 0:E], gate_in[:, :], ident[0:E, 0:E]).then_inc(gate_psum, 1)

            pe.wait_ge(w_loaded, 16 * 2 * 3)
            for i in range(2 * (E + 1)):
                at_least(pe, wL_done, i - 2)
                for c in range(HC):
                    w_in = (w1_in, w2_in)[i % 2][:, (i // 2) * H + c * P:(i // 2) * H + (c + 1) * P]
                    last = pe.transpose(ps_w[i % 3][:, c * P:(c + 1) * P], w_in, ident[:, :])
                last.then_inc(w_psum, 1)
            pe.wait_ge(nTL_done, GROUPS)
            pe.wait_ge(route, 2)
            for t in range(TILES):
                cols = slice(t * P, (t + 1) * P)
                both = ps_logit[:, t * 2 * E:(t + 1) * 2 * E]
                gate = gT[:, :, :].rearrange("p k e -> p (k e)")
                pe.matmul(both, nTH[:, cols], gate, start=True, stop=False)
                last = pe.matmul(both, nTL[:, cols], gate, start=False, stop=True)
            last.then_inc(logit_psum, 1)

            def shared_up(s, c):
                i = HC * s + c
                at_least(pe, sT_done, i - HC + 1)
                hold(pe, counter)
                w = slice(E * H + c * P, E * H + (c + 1) * P)
                tokens = ds(s * GW, GW)
                matmul3(ps_sup[c][:, :], w1H[:, w], w1L[:, w], nTH[:, tokens], nTL[:, tokens],
                        start=True, stop=True).then_inc(sup_psum, 1)

            def shared_down(s, c):
                i = HC * s + c
                if c == 0:
                    at_least(pe, sout_done, s)
                pe.wait_ge(sTL_done, i + 1)
                w = w2[:, E * HC + c]
                last = matmul3(ps_sout[:, :], w[:, 0], w[:, 1], sTH[c], sTL[c],
                               start=(c == 0), stop=(c == HC - 1))
                last.then_inc(sdown_done, 1)

            def shared_rows_back(s):
                pe.wait_ge(sout_done, s + 1)
                at_least(pe, shared_done, s)
                for t in range(G):
                    cols = slice(t * P, (t + 1) * P)
                    last = pe.transpose(ps_srows[:, cols], shared_T[:, cols], ident[:, :])
                last.then_inc(srows_psum, 1)

            pe.wait_ge(wL_done, 2 * (E + 1))
            def prefix_counts():
                pe.wait_ge(picked_done, 1)
                by_expert = picked[:, :, :].rearrange("p t e -> p e t")
                pe.matmul(ps_before.rearrange("p (e t) -> p e t", e=E), before[:, :], by_expert, start=True, stop=True)
                pe.matmul(ps_total.rearrange("p (e t) -> p e t", e=E), ones[:, :], by_expert, start=True, stop=True)\
                    .then_inc(prefix_psum, 1)

            run_shared(pe, shared_up, shared_down, shared_rows_back, prefix_counts)

            for i in range(K * TILES):
                if i % PAIRS == 0:
                    pe.wait_ge(onehot_done, i // PAIRS + 1)
                last = pe.matmul(ps_inverse[:, 0:2 * BLOCKS], at_lane[:, i], at_block[:, i], start=(i == 0),
                                 stop=(i == K * TILES - 1))
            last.then_inc(inverse_psum, 1)
            pe.wait_ge(tables_done, 1)
            pe.wait_ge(shared_done, GROUPS)

            def transpose_rows(r, j):
                b = RING * r + j
                pe.wait_ge(gathered[j], 16 * (r + 1))
                at_least(pe, xTL_done, b - 1)
                pe.transpose(ps_x[j % 2][:, 0:P], rows_in[:, j], ident[:, :]).then_inc(xT_psum, 1)

            weight_reg = [pe.alloc_register(f"weight_reg{i}") for i in range(4)]

            def set_weights(r, j):
                pe.reg_load(weight_reg[j % 4], weight_at[0:1, ds(RING * r + j, 1)])

            def weight_start(j):
                return pe.snap(weight_reg[j % 4], min_val=0, max_val=(E - 1) * H)

            def up(b, j):
                at, slot2 = weight_start(j), j % 2
                pe.wait_ge(xTL_done, b + 1)
                at_least(pe, h_done, b - 1)
                hold(pe, counter)
                matmul3(ps_up[slot2][:, :], xTH[:, slot2], xTL[:, slot2], w1H[:, ds(at, H)], w1L[:, ds(at, H)],
                        start=True, stop=True).then_inc(up_psum, 1)

            def transpose_h(b, slot2):
                pe.wait_ge(h_done, b + 1)
                at_least(pe, hTL_done, b - 1)
                for c in range(HC):
                    cols = slice(c * P, (c + 1) * P)
                    last = pe.transpose(ps_hT[slot2][:, cols], h[:, slot2, cols], ident[:, :])
                last.then_inc(hT_psum, 1)

            def down(b, j):
                at, slot2 = weight_start(j), j % 2
                pe.wait_ge(hTL_done, b + 1)
                at_least(pe, y_done, b - 1)
                hold(pe, counter)
                for c in range(HC):
                    cols = slice(c * P, (c + 1) * P)
                    chunk = w2[:, :, :, :].rearrange("p c k d -> p (c k d)")[:, ds(2 * at + c * 2 * D, 2 * D)]
                    pe.matmul(ps_y[slot2][:, 0:2 * D], hTH[:, slot2, cols], chunk, start=(c == 0), stop=False)
                    last = pe.matmul(ps_y[slot2][:, 0:2 * D], hTL[:, slot2, cols], chunk, start=False,
                                     stop=(c == HC - 1))
                last.then_inc(y_psum, 1)

            def pe_round(r, first=False, last=False):
                for j in range(RING):
                    b = RING * r + j
                    if not (last and j + 2 >= RING):
                        transpose_rows(*((r, j + 2) if j + 2 < RING else (r + 1, j + 2 - RING)))
                    if not (last and j + 1 >= RING):
                        up(b + 1, j + 1)
                    transpose_h(b, j % 2)
                    if not (first and j == 0):
                        down(b - 1, j - 1)
                    if not (last and j + 2 >= RING):
                        set_weights(*((r, j + 2) if j + 2 < RING else (r + 1, j + 2 - RING)))

            transpose_rows(0, 0)
            transpose_rows(0, 1)
            set_weights(0, 0)
            set_weights(0, 1)
            up(0, 0)
            pe_round(0, first=True)
            with pe.Fori(1, ROUNDS - 1) as r:
                pe_round(r)
            pe_round(ROUNDS - 1, last=True)
            down(BLOCKS - 1, RING - 1)


_INS = ["x", "ctx_1024", "g_xattn", "g_ffn", "L0_ffn_shared_w1", "L0_ffn_shared_w2", "L0_ffn_experts_w1",
        "L0_ffn_experts_w2", "L0_ffn_gate_w"]


def kernel(**inputs):
    import numpy as np
    import concourse.bacc as bacc
    from concourse.bass_utils import run_bass_kernel_spmd

    nc = bacc.Bacc("TRN2", target_bir_lowering=False, num_devices=1)
    arrays, args = {}, []
    for name in _INS:
        a = np.ascontiguousarray(inputs[name])
        arrays[f"in_{name}"] = a
        args.append(nc.dram_tensor(f"in_{name}", a.shape, mybir.dt.from_np(a.dtype), kind="ExternalInput").ap())
    out = nc.dram_tensor("out", inputs["x"].shape, mybir.dt.float32, kind="ExternalOutput").ap()
    flamingo_gated_moe(nc, *args, out)
    r = run_bass_kernel_spmd(nc, [arrays], core_ids=[0])
    return r.results[0]["out"]
```

```python
import concourse.bass as bass
from concourse import mybir
from contextlib import ExitStack


def flamingo_gated_moe(nc, x, ctx, g_xattn, g_ffn, sw1, sw2, ew1, ew2, gate_w, out):
    f32 = mybir.dt.float32
    f32r = mybir.dt.float32r
    bf16 = mybir.dt.bfloat16
    i32 = mybir.dt.int32
    ALU = mybir.AluOpType
    ACT = mybir.ActivationFunctionType
    AX = mybir.AxisListType.X
    ds = bass.ds

    P = 128
    B, S, D = x.shape
    H = sw1.shape[0]
    E = gate_w.shape[0]
    K = 2
    T = B * S
    TILES = T // P
    HC = H // P
    G = 4
    GROUPS = TILES // G
    GW = G * D
    EPS = 1e-5
    UNITS = 2 * (E + 1)
    EARLY = 3
    TAIL = -1
    Y_SLOTS = 4
    WEIGHT_PARTS = 4
    LAGS = 4
    USED = (K * T + E * (P - 1)) // P
    RING = 8
    AHEAD = 6
    BLOCKS = -(-USED // RING) * RING
    ROUNDS = BLOCKS // RING
    LAST = USED - RING * (ROUNDS - 1)
    P_SHIFT = P.bit_length() - 1
    FAR = -3.0e38
    PAIRS = 16
    PARTS = K * TILES // PAIRS

    x_rows = x.rearrange("b s d -> (b s) d").rearrange("(t p) d -> p t d", p=P)
    ctx_rows = ctx.rearrange("b s d -> (b s) d").rearrange("(t p) d -> p t d", p=P)
    out_rows = out.rearrange("b s d -> (b s) d").rearrange("(t p) d -> p t d", p=P)

    ew1_rows = ew1.rearrange("e (c p) d -> p (e c) d", p=P)
    ew2_rows = ew2.rearrange("e d h -> d e h")

    stack = ExitStack()
    with stack:
        def sb(name, shape, dt=f32):
            return stack.enter_context(nc.sbuf_tensor(name, shape, dt))

        def sem(name):
            return stack.enter_context(nc.semaphore(name))

        n_dram = nc.dram_tensor("n_rows", (T, D), f32, kind="Internal").ap()
        y_dram = nc.dram_tensor("y_rows", (K * T + BLOCKS * P, D), f32, kind="Internal").ap()
        n_rows = n_dram.rearrange("(t p) d -> p t d", p=P)
        y_by_choice = y_dram[0:K * T, :].rearrange("(k t p) d -> p k t d", p=P, k=K)

        xres = sb("xres", [P, TILES * D])
        nTH = sb("nTH", [D, T], f32r)
        nTL = sb("nTL", [D, T], f32r)
        w1H = sb("w1H", [D, (E + 1) * H], f32r)
        w1L = sb("w1L", [D, (E + 1) * H], f32r)
        w2 = sb("w2", [P, (E + 1) * HC, 2, D], f32r)
        w1_in = sb("w1_in", [P, (E + 1) * HC * D])
        w2_in = sb("w2_in", [D, (E + 1) * H])
        gate_in = sb("gate_in", [E, D])
        gT = sb("gT", [D, 2, E], f32r)
        ident = sb("ident", [P, P])
        mask = sb("mask", [P, P])
        ident4 = sb("ident4", [P, G, P], bf16)
        before = sb("before", [P, P], bf16)
        ones = sb("ones", [P, P], bf16)
        lane_row = sb("lane_row", [P, P], bf16)
        block_row = sb("block_row", [P, BLOCKS], bf16)
        block_start = sb("block_start", [1, BLOCKS])
        lane = sb("lane", [P, 1])
        pad_row = sb("pad_row", [P, BLOCKS])
        rev_expert = sb("rev_expert", [P, E])
        tanh_g = sb("tanh_g", [P, 2])
        ctx_in = sb("ctx_in", [P, 2, GW])
        stats = sb("stats", [P, 2, 2, G, 6])
        mv1 = sb("mv1", [P, 2, G, 2])
        rstd1 = sb("rstd1", [P, 2, G])
        mv2 = sb("mv2", [P, 2, G, 2])
        rstd2 = sb("rstd2", [P, 2, G])
        shift2 = sb("shift2", [P, 2, G])
        unused = sb("unused", [P, 3])
        minus_half = sb("minus_half", [P, G])
        neg_mean = sb("neg_mean", [P, 2, G])
        q = sb("q", [P, 2, GW])
        kT = sb("kT", [D, 2, GW])
        scores = sb("scores", [P, 2, GW])
        n = sb("n", [P, 2, GW])
        cells = E * TILES
        spare = [t[:, j, c * cells:(c + 1) * cells] for t in (kT, scores) for j in range(2) for c in range(GW // cells)]
        spare += [n[:, 1, c * cells:(c + 1) * cells] for c in range(GW // cells)]
        logit, work, work2, *pick = (v.rearrange("p (t e) -> p t e", e=E) for v in spare[:3 + K])
        total, upto, where, restart = (v.rearrange("p (e t) -> p e t", t=TILES) for v in spare[3 + K:7 + K])
        best = sb("best", [P, K, TILES])
        rank = sb("rank", [P, TILES])
        logit_high = spare[7 + K].rearrange("p (t e) -> p t e", e=E)
        picked = sb("picked", [P, TILES, E], bf16)
        count_i = sb("count_i", [P, E], i32)
        padded = sb("padded", [P, E])
        upto_e = sb("upto_e", [P, E])
        ones_e = sb("ones_e", [P, E])
        start_e = sb("start_e", [P, E])
        passed = sb("passed", [1, BLOCKS, E])
        expert_f = sb("expert_f", [1, BLOCKS])
        weight_at = sb("weight_at", [1, BLOCKS], i32)
        slot = sb("slot", [P, K, TILES])
        slot_i = sb("slot_i", [P, K * TILES], i32)
        slot_lane_i = sb("slot_lane_i", [P, K * TILES], i32)
        slot_block_i = sb("slot_block_i", [P, K * TILES], i32)
        slot_lane = sb("slot_lane", [P, K * TILES])
        slot_block = sb("slot_block", [P, K * TILES])
        gate_e = sb("gate_e", [P, TILES])
        gate_d = sb("gate_d", [P, TILES])
        gates = sb("gates", [P, K, TILES])
        at_lane = w1_in[:, 0:K * TILES * P // 2].bitcast(bf16).rearrange("p (i d) -> p i d", d=P)
        at_block = w2_in[:, 0:K * TILES * BLOCKS].bitcast(bf16).rearrange("p (i d) -> p i d", d=2 * BLOCKS)
        inverse = sb("inverse", [P, 2 * BLOCKS])
        is_pad = sb("is_pad", [P, BLOCKS])
        dest_f = sb("dest_f", [P, BLOCKS])
        dest = sb("dest", [P, BLOCKS], i32)
        source = sb("source", [P, BLOCKS], i32)
        source_now = sb("source_now", [P, RING], i32)
        dest_now = sb("dest_now", [P, RING], i32)
        xTH = sb("xTH", [D, 2, P], f32r)
        xTL = sb("xTL", [D, 2, P], f32r)
        hTH = sb("hTH", [P, 2, HC * P], f32r)
        hTL = sb("hTL", [P, 2, HC * P], f32r)
        more_sTH = sb("more_sTH", [P, 2, G * P], f32r)
        more_sTL = sb("more_sTL", [P, 2, G * P], f32r)
        h = w2_in[:, 0:2 * H].rearrange("p (s h) -> p s h", s=2)
        rows_in = w2_in[:, 6 * H:6 * H + RING * D].rearrange("p (s d) -> p s d", s=RING)
        y = w2_in[:, 2 * H:2 * H + RING * D].rearrange("p (s d) -> p s d", s=RING)
        y_low = w2_in[:, 5 * H:5 * H + 2 * D].rearrange("p (s d) -> p s d", s=2)
        sT = [ctx_in[:, 0], ctx_in[:, 1], q[:, 0], q[:, 1]]
        shared_T = n[:, 0]
        sTH = [hTH[:, 0], hTH[:, 1], more_sTH[:, 0], more_sTH[:, 1]]
        sTL = [hTL[:, 0], hTL[:, 1], more_sTL[:, 0], more_sTL[:, 1]]
        y_in = w1_in[:, 0:Y_SLOTS * K * GW].rearrange("p (j k d) -> p j k d", j=Y_SLOTS, k=K)

        bank = [stack.enter_context(nc.psum_tensor(f"bank{i}", [P, 512], f32)) for i in range(8)]
        ps_k, ps_s, ps_q, ps_n, ps_logit = bank[0], bank[1], bank[2], bank[3], bank[4]
        ps_w = [bank[5], bank[6], bank[7]]
        ps_gate = bank[7]
        ps_before, ps_total, ps_inverse = bank[4][:, 0:cells], bank[4][:, cells:2 * cells], bank[4]
        ps_sup, ps_sout, ps_srows = [bank[3], bank[5], bank[6], bank[7]], [bank[0], bank[2]], bank[1]
        ps_x, ps_up = [bank[0], bank[7]], [bank[1], bank[2]]
        ps_hT, ps_y = [bank[3], bank[4]], [bank[5], bank[6]]

        pool_holds = sem("pool_holds")
        act_holds = sem("act_holds")
        dve_holds = sem("dve_holds")
        pe_holds = sem("pe_holds")
        consts_ready = sem("consts_ready")
        pool_steps = sem("pool_steps")
        small_in = sem("small_in")
        x_in = [sem(f"x_in{i}") for i in range(3)]
        ctx_loaded = [sem(f"ctx_loaded{j}") for j in range(2)]
        w_loaded = [sem(f"w_loaded{j}") for j in range(1 + WEIGHT_PARTS)]
        tanh_done = sem("tanh_done")
        kT_psum = sem("kT_psum")
        kT_done = sem("kT_done")
        s_psum = sem("s_psum")
        scores_done = sem("scores_done")
        stats1_part = sem("stats1_part")
        stats1_done = sem("stats1_done")
        centred_done = sem("centred_done")
        q_done = sem("q_done")
        attn_psum = sem("attn_psum")
        x1_done = sem("x1_done")
        rstd1_part = sem("rstd1_part")
        rstd1_done = sem("rstd1_done")
        scale2_part = sem("scale2_part")
        scale2_done = sem("scale2_done")
        stats2_part = sem("stats2_part")
        stats2_done = sem("stats2_done")
        n_done = sem("n_done")
        n_stored = [sem(f"n_stored{j}") for j in range(2)]
        nT_psum = sem("nT_psum")
        nTH_done = sem("nTH_done")
        nTL_done = sem("nTL_done")
        gate_psum = sem("gate_psum")
        w_psum = sem("w_psum")
        wH_done = sem("wH_done")
        wL_done = sem("wL_done")
        logit_psum = sem("logit_psum")
        route = sem("route")
        gate_exp = sem("gate_exp")
        picked_done = sem("picked_done")
        prefix_psum = sem("prefix_psum")
        onehot_part = sem("onehot_part")
        onehot_done = sem("onehot_done")
        inverse_psum = sem("inverse_psum")
        gate_gap_done = sem("gate_gap_done")
        gates_done = sem("gates_done")
        tables_done = sem("tables_done")
        source_set = sem("source_set")
        dest_set = sem("dest_set")
        gathered = [sem(f"gathered{j}") for j in range(RING)]
        scattered = [sem(f"scattered{j}") for j in range(RING)]
        xT_psum = sem("xT_psum")
        xTH_done = sem("xTH_done")
        xTL_done = sem("xTL_done")
        up_psum = sem("up_psum")
        h_done = sem("h_done")
        hT_psum = sem("hT_psum")
        hTH_done = sem("hTH_done")
        hTL_done = sem("hTL_done")
        y_psum = sem("y_psum")
        y_done = sem("y_done")
        y_low_done = sem("y_low_done")
        sup_psum = sem("sup_psum")
        sT_done = sem("sT_done")
        sTH_done = sem("sTH_done")
        sTL_done = sem("sTL_done")
        sdown_done = sem("sdown_done")
        sout_done = sem("sout_done")
        srows_psum = sem("srows_psum")
        shared_done = sem("shared_done")
        scaled_done = sem("scaled_done")
        y_loaded = [sem(f"y_loaded{j}") for j in range(Y_SLOTS)]
        half_done = sem("half_done")
        out_done = sem("out_done")
        stored = sem("stored")

        def at_least(eng, semaphore, value):
            if not (isinstance(value, int) and value <= 0):
                eng.wait_ge(semaphore, value)

        def hold(eng, counter):
            eng.sem_inc(counter, 1)

        def run_phase_a(eng, *stages):
            steps = GROUPS + LAGS
            head, tail = 4, GROUPS

            def step(half, j):
                for lag, stage in stages:
                    if lag == TAIL:
                        if isinstance(half, int) and 2 * half + j >= tail:
                            stage(2 * half + j - tail)
                    elif isinstance(half, int):
                        g = 2 * half + j - lag
                        if 0 <= g < GROUPS:
                            stage(g // 2, g % 2)
                    else:
                        stage(half - (lag - j + 1) // 2, (j - lag) % 2)

            for i in range(head):
                step(i // 2, i % 2)
            with eng.Fori(head // 2, tail // 2) as half:
                step(half, 0)
                step(half, 1)
            for i in range(tail, steps):
                step(i // 2, i % 2)

        def shared_group(up, down, s, parity, rows_back=None, before_down=None, last=False):
            for c in range(HC):
                if c + 3 < HC:
                    up(s, c + 3)
                elif not last:
                    up(s + 1, c + 3 - HC)
                if c == 0 and before_down:
                    before_down()
                down(s, c, parity)
                if c == 0 and rows_back:
                    rows_back(s - 1)

        def run_shared(eng, up, down, rows_back=None, prefix=None, invert=None):
            for c in range(3):
                up(0, c)
            shared_group(up, down, 0, 0)
            if prefix:
                prefix()
            shared_group(up, down, 1, 1, rows_back)
            with eng.Fori(1, GROUPS // 2 - 2) as half:
                shared_group(up, down, 2 * half, 0, rows_back)
                shared_group(up, down, 2 * half + 1, 1, rows_back)
            shared_group(up, down, GROUPS - 4, 0, rows_back)
            shared_group(up, down, GROUPS - 3, 1, rows_back, before_down=invert and (lambda: invert(0)))
            shared_group(up, down, GROUPS - 2, 0, rows_back, before_down=invert and (lambda: invert(1)), last=True)
            if rows_back:
                rows_back(GROUPS - 2)

        def run_last_shared(up, down, rows_back=None):
            for c in range(3):
                up(GROUPS - 1, c)
            shared_group(up, down, GROUPS - 1, 1, last=True)
            if rows_back:
                rows_back(GROUPS - 1)

        block = stack.enter_context(nc.Block())

        @block.sync
        def _(sp):

            def load_ctx(qq, j):
                at_least(sp, kT_psum, 2 * qq + j - 1)
                sp.dma_start(ctx_in[:, j].rearrange("p (t d) -> p t d", d=D),
                             ctx_rows[:, ds((2 * qq + j) * G, G), :]).then_inc(ctx_loaded[j], 16)

            def store_n(qq, j):
                g = 2 * qq + j
                sp.wait_ge(n_done, G * (g + 1))
                sp.dma_start(n_rows[:, ds(g * G, G), :],
                             n[:, j].rearrange("p (t d) -> p t d", d=D)).then_inc(n_stored[j], 16)

            load_ctx(0, 0)
            for part, (a, b) in enumerate(((0, G), (G, 2 * G), (2 * G, TILES))):
                sp.dma_start(xres[:, a * D:b * D].rearrange("p (t d) -> p t d", d=D),
                             x_rows[:, a:b, :]).then_inc(x_in[part], 16)
                if part == 0:
                    load_ctx(0, 1)
                elif part == 1:
                    sp.dma_start(tanh_g[:, 0:1], g_xattn.rearrange("(a n) -> a n", a=1).to_broadcast([P, 1]))\
                        .then_inc(small_in, 16)
                    sp.dma_start(tanh_g[:, 1:2], g_ffn.rearrange("(a n) -> a n", a=1).to_broadcast([P, 1]))\
                        .then_inc(small_in, 16)
                    sp.dma_start(gate_in[:, :], gate_w).then_inc(small_in, 16)

            def load_shared():
                sp.dma_start(w1_in[:, E * H:].rearrange("p (c d) -> p c d", d=D),
                             sw1.rearrange("(c p) d -> p c d", p=P)).then_inc(w_loaded[0], 16)
                sp.dma_start(w2_in[:, E * H:], sw2).then_inc(w_loaded[0], 16)

            def load_experts(part):
                count = E // WEIGHT_PARTS
                first = part * count
                loaded = w_loaded[1 + part]
                sp.dma_start(w1_in[:, first * H:(first + count) * H].rearrange("p (a d) -> p a d", d=D),
                             ew1_rows[:, first * HC:(first + count) * HC, :]).then_inc(loaded, 16)
                sp.dma_start(w2_in[:, first * H:(first + count) * H].rearrange("p (e h) -> p e h", h=H),
                             ew2_rows[:, first:first + count, :]).then_inc(loaded, 16)

            for g in range(2, GROUPS + LAGS):
                if g < GROUPS:
                    load_ctx(g // 2, g % 2)
                if g >= LAGS:
                    store_n((g - LAGS) // 2, (g - LAGS) % 2)
                if g == 2:
                    load_shared()
                elif g - 3 < WEIGHT_PARTS:
                    load_experts(g - 3)

            for j in range(RING):
                sp.wait_ge(scattered[j], 16 * (ROUNDS if j < LAST else ROUNDS - 1))

            def load_y(r, j):
                at_least(sp, out_done, Y_SLOTS * (r - 1) + j + 1)
                for k in range(K):
                    sp.dma_start(y_in[:, j, k].rearrange("p (t d) -> p t d", d=D),
                                 y_by_choice[:, k, ds((Y_SLOTS * r + j) * G, G), :]).then_inc(y_loaded[j], 16)

            def store_out(r, j):
                g = Y_SLOTS * r + j
                sp.wait_ge(out_done, g + 1)
                sp.dma_start(out_rows[:, ds(g * G, G), :],
                             xres[:, ds(g * GW, GW)].rearrange("p (t d) -> p t d", d=D)).then_inc(stored, 16)

            for j in range(Y_SLOTS):
                load_y(0, j)
            with sp.Fori(1, GROUPS // Y_SLOTS) as r:
                for j in range(Y_SLOTS):
                    load_y(r, j)
                    store_out(r - 1, j)
            for j in range(Y_SLOTS):
                store_out(GROUPS // Y_SLOTS - 1, j)
            sp.wait_ge(stored, 16 * GROUPS)

        @block.gpsimd
        def _(pool):
            counter = pool_holds
            step = [0]

            def chained(instruction):
                step[0] += 1
                instruction.then_inc(pool_steps, 1)
                pool.wait_ge(pool_steps, step[0])

            chained(pool.memset(ident[:, :], 0.0))
            chained(pool.affine_select(out=ident[:, :], in_=ident[:, :], compare_op=ALU.not_equal, fill=1.0,
                                       base=0, pattern=[[-1, P]], channel_multiplier=1))
            pool.memset(unused[:, 0:1], 0.0).then_inc(consts_ready, 1)
            chained(pool.memset(ident4[:, :, :], 0.0))
            chained(pool.affine_select(out=ident4[:, :, :], in_=ident4[:, :, :], compare_op=ALU.not_equal, fill=1.0,
                                       base=0, pattern=[[0, G], [-1, P]], channel_multiplier=1))
            chained(pool.memset(mask[:, :], 1.0))
            chained(pool.affine_select(out=mask[:, :], in_=mask[:, :], compare_op=ALU.is_ge, fill=0.0,
                                       base=0, pattern=[[1, P]], channel_multiplier=-1))
            chained(pool.affine_select(out=mask[:, S:P], in_=mask[:, S:P], compare_op=ALU.is_ge, fill=0.0,
                                       base=-S, pattern=[[0, P - S]], channel_multiplier=1))
            chained(pool.memset(minus_half[:, :], -0.5))
            pool.memset(unused[:, 1:2], 0.0).then_inc(consts_ready, 1)

            def centre_and_scale(qq, j):
                g = 2 * qq + j
                xg = xres[:, ds(g * GW, GW)].rearrange("p (t d) -> p t d", d=D)
                at_least(pool, attn_psum, g - 1)
                pool.wait_ge(stats1_done, g + 1)
                hold(pool, counter)
                pool.tensor_scalar(rstd1[:, j], mv1[:, j, :, 1], EPS, None, ALU.add).then_inc(rstd1_part, 1)
                pool.wait_ge(rstd1_part, g + 1)
                pool.tensor_tensor(rstd1[:, j], rstd1[:, j], minus_half[:, :], ALU.pow).then_inc(rstd1_done, 1)
                pool.tensor_tensor(q[:, j].rearrange("p (t d) -> p t d", d=D), xg,
                                   mv1[:, j, :, 0:1].to_broadcast([P, G, D]), ALU.subtract).then_inc(centred_done, 1)
                pool.wait_ge(rstd1_done, g + 1)
                hold(pool, counter)
                pool.wait_ge(centred_done, g + 1)
                pool.tensor_tensor(q[:, j].rearrange("p (t d) -> p t d", d=D),
                                   q[:, j].rearrange("p (t d) -> p t d", d=D),
                                   rstd1[:, j].unsqueeze(2).to_broadcast([P, G, D]), ALU.mult).then_inc(q_done, 1)

            def scale_and_shift(qq, j):
                g = 2 * qq + j
                at_least(pool, n_done, G * (g - 1))
                hold(pool, counter)
                pool.wait_ge(stats2_done, g + 1)
                hold(pool, counter)
                pool.tensor_scalar(rstd2[:, j], mv2[:, j, :, 1], EPS, None, ALU.add).then_inc(scale2_part, 1)
                pool.tensor_scalar(neg_mean[:, j], mv2[:, j, :, 0], -1.0, None, ALU.mult).then_inc(scale2_part, 1)
                pool.wait_ge(scale2_part, 3 * g + 2)
                pool.tensor_tensor(rstd2[:, j], rstd2[:, j], minus_half[:, :], ALU.pow).then_inc(scale2_part, 1)
                pool.wait_ge(scale2_part, 3 * g + 3)
                pool.tensor_tensor(shift2[:, j], neg_mean[:, j], rstd2[:, j], ALU.mult).then_inc(scale2_done, 1)

            run_phase_a(pool, (0, centre_and_scale), (2, scale_and_shift))

            chained(pool.memset(before[:, :], 1.0))
            chained(pool.affine_select(out=before[:, :], in_=before[:, :], compare_op=ALU.is_gt, fill=0.0,
                                       base=0, pattern=[[1, P]], channel_multiplier=-1))
            chained(pool.memset(ones[:, :], 1.0))
            chained(pool.memset(ones_e[:, :], 1.0))
            chained(pool.iota(lane_row[:, :], pattern=[[1, P]], base=0, channel_multiplier=0,
                              allow_small_or_imprecise_dtypes=True))
            chained(pool.iota(block_row[:, :], pattern=[[1, BLOCKS]], base=0, channel_multiplier=0,
                              allow_small_or_imprecise_dtypes=True))
            chained(pool.iota(block_start[:, :], pattern=[[P, BLOCKS]], base=0, channel_multiplier=0,
                              allow_small_or_imprecise_dtypes=True))
            chained(pool.iota(lane[:, :], pattern=[[0, 1]], base=0, channel_multiplier=1,
                              allow_small_or_imprecise_dtypes=True))
            chained(pool.iota(pad_row[:, :], pattern=[[P, BLOCKS]], base=K * T + P, channel_multiplier=1,
                              allow_small_or_imprecise_dtypes=True))
            chained(pool.iota(rev_expert[:, :], pattern=[[-1, E]], base=E, channel_multiplier=0,
                              allow_small_or_imprecise_dtypes=True))
            pool.memset(unused[:, 2:3], 0.0).then_inc(consts_ready, 1)

            def shared_low_part(s, c):
                i = HC * s + c
                at_least(pool, sdown_done, i - HC + 1)
                hold(pool, counter)
                pool.wait_ge(sTH_done, i + 1)
                pool.tensor_tensor(sTL[c], sT[c], sTH[c].bitcast(f32), ALU.subtract)\
                    .then_inc(sTL_done, 1)

            run_shared(pool, shared_low_part, lambda s, c, parity: None)

            def gather(r, j):
                b = RING * r + j
                pool.wait_ge(source_set, b + 1)
                hold(pool, counter)
                if not (isinstance(b, int) and b < RING):
                    pool.wait_ge(xT_psum, b - RING + 1)
                    hold(pool, counter)
                pool.indirect_dma_start(out=rows_in[:, j], out_offset=None, in_=n_dram[:, :],
                                        in_offset=bass.IndirectOffsetOnAxis(ap=source_now[:, j:j + 1], axis=0))\
                    .then_inc(gathered[j], 16)

            def scatter(r, j):
                b = RING * r + j
                pool.wait_ge(y_done, b + 1)
                hold(pool, counter)
                pool.indirect_dma_start(out=y_dram[:, :],
                                        out_offset=bass.IndirectOffsetOnAxis(ap=dest_now[:, j:j + 1], axis=0),
                                        in_=y[:, j], in_offset=None).then_inc(scattered[j], 16)

            pool.wait_ge(inverse_psum, 1)
            for j in range(2):
                pool.wait_ge(n_stored[j], 16 * (GROUPS // 2))
            for j in range(RING):
                gather(0, j)
            with pool.Fori(1, ROUNDS - 1) as r:
                for j in range(RING):
                    gather(r, j)
                    scatter(r - 1, j)
            for j in range(RING):
                if j < LAST:
                    gather(ROUNDS - 1, j)
                scatter(ROUNDS - 2, j)
            for j in range(LAST):
                scatter(ROUNDS - 1, j)

            run_last_shared(shared_low_part, lambda s, c, parity: None)

            def add_second(r, j):
                g = Y_SLOTS * r + j
                pool.wait_ge(scaled_done, G * (g + 1))
                hold(pool, counter)
                pool.wait_ge(half_done, G * (g + 1))
                hold(pool, counter)
                cols = ds(g * GW, GW)
                pool.tensor_tensor(xres[:, cols], xres[:, cols], y_in[:, j, 1], ALU.add).then_inc(out_done, 1)

            with pool.Fori(0, GROUPS // Y_SLOTS) as r:
                for j in range(Y_SLOTS):
                    add_second(r, j)

        @block.scalar
        def _(act):
            counter = act_holds
            act.preload_act_table(ACT.Silu)
            act.wait_ge(small_in, 48)
            act.activation(tanh_g[:, :], tanh_g[:, :], ACT.Tanh).then_inc(tanh_done, 1)

            def evacuate_kT(qq, j):
                g = 2 * qq + j
                at_least(act, s_psum, g - 1)
                act.wait_ge(kT_psum, g + 1)
                act.activation(kT[:, j], ps_k[:, :], ACT.Copy).then_inc(kT_done, 1)

            def normalise(qq, j):
                g = 2 * qq + j
                at_least(act, n_stored[j], 16 * qq)
                at_least(act, nT_psum, g - 1)
                act.wait_ge(scale2_done, g + 1)
                hold(act, counter)
                for t in range(G):
                    act.activation(n[:, j, t * D:(t + 1) * D], xres[:, ds(g * GW + t * D, D)], ACT.Identity,
                                   bias=shift2[:, j, t:t + 1], scale=rstd2[:, j, t:t + 1]).then_inc(n_done, 1)

            def high_part_nT(qq, j):
                g = 2 * qq + j
                act.wait_ge(nT_psum, g + 1)
                hold(act, counter)
                act.activation(nTH[:, ds(g * GW, GW)], ps_n[:, :], ACT.Copy).then_inc(nTH_done, 1)

            def weights_high(i):
                e = (i // 2 + E) % (E + 1)
                act.wait_ge(w_psum, i + 1)
                ps = ps_w[i % 3][:, :]
                if i % 2 == 0:
                    act.activation(w1H[:, e * H:(e + 1) * H], ps, ACT.Copy).then_inc(wH_done, 1)
                else:
                    act.activation(w2[:, e * HC:(e + 1) * HC, 0, :], ps.rearrange("p (c d) -> p c d", d=D),
                                   ACT.Copy).then_inc(wH_done, 1)

            def weights_early(i):
                for unit in range(EARLY * i, EARLY * (i + 1)):
                    weights_high(unit)

            run_phase_a(act, (0, evacuate_kT), (3, normalise), (4, high_part_nT), (TAIL, weights_early))
            for unit in range(EARLY * LAGS, UNITS):
                weights_high(unit)

            def shared_silu(s, c):
                i = HC * s + c
                act.wait_ge(sup_psum, i + 1)
                at_least(act, sTL_done, i - HC + 1)
                act.activation(sT[c], ps_sup[c][:, :], ACT.Silu).then_inc(sT_done, 1)
                at_least(act, sdown_done, i - HC + 1)
                act.wait_ge(sT_done, i + 1)
                act.activation(sTH[c], sT[c], ACT.Copy).then_inc(sTH_done, 1)

            def shared_scaled(s, parity):
                act.wait_ge(sdown_done, HC * (s + 1))
                at_least(act, srows_psum, s)
                act.activation(shared_T, ps_sout[parity][:, :], ACT.Copy, scale=tanh_g[:, 1:2]).then_inc(sout_done, 1)

            def shared_down(s, c, parity):
                if c == HC - 1:
                    shared_scaled(s, parity)

            for j in range(2):
                act.wait_ge(n_stored[j], 16 * (GROUPS // 2))
            run_shared(act, shared_silu, shared_down)

            def high_part_xT(b, slot2):
                act.wait_ge(xT_psum, b + 1)
                at_least(act, up_psum, b - 1)
                act.activation(xTH[:, slot2], ps_x[slot2][:, 0:P], ACT.Copy).then_inc(xTH_done, 1)

            def silu(b, slot2):
                act.wait_ge(up_psum, b + 1)
                at_least(act, hT_psum, b - 1)
                act.activation(h[:, slot2], ps_up[slot2][:, :], ACT.Silu).then_inc(h_done, 1)

            def high_part_hT(b, slot2):
                act.wait_ge(hT_psum, b + 1)
                at_least(act, y_psum, b - 1)
                act.activation(hTH[:, slot2], ps_hT[slot2][:, :], ACT.Copy).then_inc(hTH_done, 1)

            def evacuate_low_y(b, slot2):
                act.wait_ge(y_psum, b + 1)
                at_least(act, y_done, b - 1)
                act.activation(y_low[:, slot2], ps_y[slot2][:, D:2 * D], ACT.Copy).then_inc(y_low_done, 1)

            def act_round(r, first=False, last=False):
                count = LAST if last else RING
                for j in range(count):
                    b = RING * r + j
                    if not (last and j + 2 >= count):
                        high_part_xT(b + 2, j % 2)
                    if not (last and j + 1 >= count):
                        silu(b + 1, (j + 1) % 2)
                    high_part_hT(b, j % 2)
                    if not (first and j == 0):
                        evacuate_low_y(b - 1, (j - 1) % 2)

            high_part_xT(0, 0)
            high_part_xT(1, 1)
            silu(0, 0)
            act_round(0, first=True)
            with act.Fori(1, ROUNDS - 1) as r:
                act_round(r)
            act_round(ROUNDS - 1, last=True)
            evacuate_low_y(USED - 1, (LAST - 1) % 2)

            act.wait_ge(gate_gap_done, 1)
            act.activation(gate_e[:, :], gate_d[:, :], ACT.Exp).then_inc(gate_exp, 1)
            act.preload_act_table(ACT.Silu)

            run_last_shared(shared_silu, lambda s, c, parity: None)

            def scale_second(r, j):
                g = Y_SLOTS * r + j
                act.wait_ge(y_loaded[j], 16 * K * (r + 1))
                hold(act, counter)
                for t in range(G):
                    cols = slice(t * D, (t + 1) * D)
                    act.activation(y_in[:, j, 1, cols], y_in[:, j, 1, cols], ACT.Copy,
                                   scale=gates[:, 1, ds(g * G + t, 1)]).then_inc(scaled_done, 1)

            act.wait_ge(gates_done, 1)
            with act.Fori(0, GROUPS // Y_SLOTS - 1) as r:
                for j in range(Y_SLOTS):
                    scale_second(r, j)
            shared_scaled(GROUPS - 1, 1)
            for j in range(Y_SLOTS):
                scale_second(GROUPS // Y_SLOTS - 1, j)

        @block.vector
        def _(dve):
            counter = dve_holds
            step = [0]

            def chained(instruction):
                step[0] += 1
                instruction.then_inc(route, 1)
                dve.wait_ge(route, step[0])

            def mean_variance(src, mv, which, j, part, before_parts):
                for t in range(G):
                    dve.bn_stats(stats[:, which, j, t, :], src(t)).then_inc(part, 1)
                dve.wait_ge(part, before_parts + G)
                hold(dve, counter)
                for t in range(G):
                    last = dve.bn_aggr(mv[:, j, t, :], stats[:, which, j, t, :])
                return last

            def statistics(qq, j):
                g = 2 * qq + j
                if isinstance(qq, int):
                    dve.wait_ge(x_in[min(g, 2)], 16)
                else:
                    dve.wait_ge(x_in[2], 16)
                at_least(dve, q_done, g - 1)
                hold(dve, counter)
                mean_variance(lambda t: xres[:, ds(g * GW + t * D, D)], mv1, 0, j, stats1_part, G * g)\
                    .then_inc(stats1_done, 1)

            def mask_scores(qq, j):
                g = 2 * qq + j
                if isinstance(qq, int) and g == 0:
                    dve.wait_ge(consts_ready, 2)
                at_least(dve, attn_psum, g - 1)
                dve.wait_ge(s_psum, g + 1)
                dve.tensor_tensor(scores[:, j].rearrange("p (t d) -> p t d", d=P),
                                  ps_s[:, :].rearrange("p (t d) -> p t d", d=P),
                                  mask[:, :].unsqueeze(1).to_broadcast([P, G, P]), ALU.mult).then_inc(scores_done, 1)

            def residual(qq, j):
                g = 2 * qq + j
                if isinstance(qq, int) and g == 0:
                    dve.wait_ge(tanh_done, 1)
                dve.wait_ge(attn_psum, g + 1)
                dve.scalar_tensor_tensor(out=xres[:, ds(g * GW, GW)], in0=ps_q[:, :], scalar=tanh_g[:, 0:1],
                                         in1=xres[:, ds(g * GW, GW)], op0=ALU.mult, op1=ALU.add).then_inc(x1_done, 1)
                dve.wait_ge(x1_done, g + 1)
                hold(dve, counter)
                at_least(dve, n_done, G * (g - 1))
                hold(dve, counter)
                mean_variance(lambda t: xres[:, ds(g * GW + t * D, D)], mv2, 1, j, stats2_part, G * g)\
                    .then_inc(stats2_done, 1)

            def low_part_nT(qq, j):
                g = 2 * qq + j
                dve.wait_ge(nTH_done, g + 1)
                dve.tensor_tensor(nTL[:, ds(g * GW, GW)], ps_n[:, :], nTH[:, ds(g * GW, GW)].bitcast(f32),
                                  ALU.subtract).then_inc(nTL_done, 1)

            def gate_parts(i):
                if i == 0:
                    dve.wait_ge(gate_psum, 1)
                    chained(dve.tensor_copy(gT[:, 0], ps_gate[:, 0:E]))
                    chained(dve.tensor_tensor(gT[:, 1], ps_gate[:, 0:E], gT[:, 0].bitcast(f32), ALU.subtract))

            def weights_low(i):
                e = (i // 2 + E) % (E + 1)
                dve.wait_ge(wH_done, i + 1)
                ps = ps_w[i % 3][:, :]
                if i % 2 == 0:
                    cols = slice(e * H, (e + 1) * H)
                    dve.tensor_tensor(w1L[:, cols], ps, w1H[:, cols].bitcast(f32), ALU.subtract).then_inc(wL_done, 1)
                else:
                    rows = slice(e * HC, (e + 1) * HC)
                    dve.tensor_tensor(w2[:, rows, 1, :], ps.rearrange("p (c d) -> p c d", d=D),
                                      w2[:, rows, 0, :].bitcast(f32), ALU.subtract).then_inc(wL_done, 1)

            def weights_early(i):
                for unit in range(EARLY * i, EARLY * (i + 1)):
                    weights_low(unit)

            run_phase_a(dve, (TAIL, gate_parts), (0, statistics), (1, mask_scores), (2, residual), (4, low_part_nT),
                        (TAIL, weights_early))

            for unit in range(EARLY * LAGS, UNITS):
                weights_low(unit)

            def add_shared(s):
                dve.wait_ge(srows_psum, s + 1)
                cols = slice(s * GW, (s + 1) * GW)
                dve.tensor_tensor(xres[:, cols], ps_srows[:, :], xres[:, cols], ALU.add).then_inc(shared_done, 1)

            dve.wait_ge(logit_psum, GROUPS)
            dve.wait_ge(consts_ready, 3)
            dve.wait_ge(n_stored[1], 16 * (GROUPS // 2))
            chained(dve.memset(restart[:, :, :], 1.0))
            chained(dve.memset(restart[:, :, 0:1], 0.0))
            logit_parts = ps_logit[:, :].rearrange("p (t k e) -> p t k e", k=2, e=E)
            chained(dve.tensor_copy(logit_high[:, :, :], logit_parts[:, :, 0, :]))
            chained(dve.tensor_tensor(logit[:, :, :], logit_parts[:, :, 1, :], logit_high[:, :, :], ALU.add))
            rev = rev_expert[:, :].unsqueeze(1).to_broadcast([P, TILES, E])
            left = logit
            for k in range(K):
                top = best[:, k].unsqueeze(2)
                chained(dve.tensor_reduce(best[:, k], left[:, :, :], AX, ALU.max))
                chained(dve.tensor_tensor(work[:, :, :], left[:, :, :], top.to_broadcast([P, TILES, E]), ALU.is_equal))
                chained(dve.tensor_tensor(work[:, :, :], work[:, :, :], rev, ALU.mult))
                chained(dve.tensor_reduce(rank[:, :], work[:, :, :], AX, ALU.max))
                chained(dve.tensor_tensor(pick[k][:, :, :], rank[:, :].unsqueeze(2).to_broadcast([P, TILES, E]), rev,
                                          ALU.is_equal))
                if k == 0:
                    chained(dve.scalar_tensor_tensor(out=work2[:, :, :], in0=pick[0][:, :, :], scalar=FAR,
                                                     in1=logit[:, :, :], op0=ALU.mult, op1=ALU.add))
                    left = work2
            dve.tensor_tensor(gate_d[:, :], best[:, 1], best[:, 0], ALU.subtract).then_inc(gate_gap_done, 1)
            dve.tensor_tensor(picked[:, :, :], pick[0][:, :, :], pick[1][:, :, :], ALU.add).then_inc(picked_done, 1)
            dve.wait_ge(prefix_psum, 1)
            by_expert = "p (e t) -> p e t"
            chained(dve.tensor_copy(total[:, :, :], ps_total.rearrange(by_expert, t=TILES)))
            chained(dve.tensor_tensor_scan(upto[:, :, :].rearrange("p e t -> p (e t)"),
                                           restart[:, :, :].rearrange("p e t -> p (e t)"),
                                           total[:, :, :].rearrange("p e t -> p (e t)"), 0.0, ALU.mult, ALU.add))
            chained(dve.tensor_scalar(count_i[:, :], upto[:, :, TILES - 1], float(P - 1), None, ALU.add))
            chained(dve.tensor_scalar(count_i[:, :], count_i[:, :], P_SHIFT, P_SHIFT, ALU.logical_shift_right,
                                      ALU.logical_shift_left))
            chained(dve.tensor_copy(padded[:, :], count_i[:, :]))
            chained(dve.tensor_tensor_scan(upto_e[:, :], ones_e[:, :], padded[:, :], 0.0, ALU.mult, ALU.add))
            chained(dve.tensor_tensor(start_e[:, :], upto_e[:, :], padded[:, :], ALU.subtract))
            chained(dve.tensor_tensor(passed[:, :, :], upto_e[0:1, :].unsqueeze(1).to_broadcast([1, BLOCKS, E]),
                                      block_start[:, :].unsqueeze(2).to_broadcast([1, BLOCKS, E]), ALU.is_le))
            chained(dve.tensor_reduce(expert_f[:, :], passed[:, :, :], AX, ALU.add))
            chained(dve.tensor_scalar(weight_at[:, :], expert_f[:, :], float(E - 1), float(H), ALU.min, ALU.mult))
            add_shared(0)
            chained(dve.tensor_tensor(where[:, :, :], upto[:, :, :], total[:, :, :], ALU.subtract))
            chained(dve.tensor_tensor(where[:, :, :], where[:, :, :],
                                      start_e[:, :].unsqueeze(2).to_broadcast([P, E, TILES]), ALU.add))
            chained(dve.tensor_tensor(where[:, :, :], where[:, :, :],
                                      ps_before.rearrange(by_expert, t=TILES), ALU.add))
            for k in range(K):
                chained(dve.tensor_tensor(work[:, :, :], where[:, :, :].rearrange("p e t -> p t e"), pick[k][:, :, :],
                                          ALU.mult))
                chained(dve.tensor_reduce(slot[:, k], work[:, :, :], AX, ALU.add))
            chained(dve.tensor_copy(slot_i[:, :], slot[:, :, :].rearrange("p k t -> p (k t)")))
            chained(dve.tensor_scalar(slot_lane_i[:, :], slot_i[:, :], P - 1, None, ALU.bitwise_and))
            chained(dve.tensor_scalar(slot_block_i[:, :], slot_i[:, :], P_SHIFT, None, ALU.logical_shift_right))
            chained(dve.tensor_copy(slot_lane[:, :], slot_lane_i[:, :]))
            chained(dve.tensor_copy(slot_block[:, :], slot_block_i[:, :]))
            add_shared(1)
            for i in range(K * TILES):
                dve.tensor_scalar(at_lane[:, i], lane_row[:, :], slot_lane[:, i:i + 1], None, ALU.is_equal)
                last = dve.tensor_scalar(at_block[:, i, 0:BLOCKS], block_row[:, :], slot_block[:, i:i + 1],
                                         float(i + 1), ALU.is_equal, ALU.mult)
                if (i + 1) % PAIRS == 0:
                    last.then_inc(onehot_part, 1)
                    some = slice(i + 1 - PAIRS, i + 1)
                    dve.wait_ge(onehot_part, i // PAIRS + 1)
                    dve.tensor_scalar(at_block[:, some, BLOCKS:], at_block[:, some, 0:BLOCKS], 0.0, lane[:, 0:1],
                                      ALU.is_gt, ALU.mult).then_inc(onehot_done, 1)
                    if (i + 1) // PAIRS < PARTS:
                        add_shared(1 + (i + 1) // PAIRS)
            dve.wait_ge(inverse_psum, 1)
            chained(dve.tensor_copy(inverse[:, :], ps_inverse[:, 0:2 * BLOCKS]))
            chained(dve.scalar_tensor_tensor(out=dest_f[:, :], in0=inverse[:, 0:BLOCKS], scalar=float(P),
                                             in1=inverse[:, BLOCKS:], op0=ALU.mult, op1=ALU.add))
            chained(dve.scalar_tensor_tensor(out=is_pad[:, :], in0=inverse[:, 0:BLOCKS], scalar=0.0,
                                             in1=pad_row[:, :], op0=ALU.is_equal, op1=ALU.mult))
            chained(dve.scalar_tensor_tensor(out=dest[:, :], in0=dest_f[:, :], scalar=-float(P), in1=is_pad[:, :],
                                             op0=ALU.add, op1=ALU.add))
            dve.tensor_scalar(source[:, :], dest[:, :], T - 1, None, ALU.bitwise_and).then_inc(tables_done, 1)
            dve.wait_ge(tables_done, 1)

            def set_source(r, j):
                at_least(dve, gathered[j], 16 * r)
                hold(dve, counter)
                dve.tensor_copy(source_now[:, j:j + 1], source[:, ds(RING * r + j, 1)]).then_inc(source_set, 1)

            def low_part_xT(b, slot2):
                dve.wait_ge(xTH_done, b + 1)
                dve.tensor_tensor(xTL[:, slot2], ps_x[slot2][:, 0:P], xTH[:, slot2].bitcast(f32), ALU.subtract)\
                    .then_inc(xTL_done, 1)

            def low_part_hT(b, slot2):
                dve.wait_ge(hTH_done, b + 1)
                dve.tensor_tensor(hTL[:, slot2], ps_hT[slot2][:, :], hTH[:, slot2].bitcast(f32), ALU.subtract)\
                    .then_inc(hTL_done, 1)

            def evacuate_y(r, j):
                b = RING * r + j
                at_least(dve, scattered[j], 16 * r)
                hold(dve, counter)
                dve.tensor_copy(dest_now[:, j:j + 1], dest[:, ds(b, 1)]).then_inc(dest_set, 1)
                dve.wait_ge(y_low_done, b + 1)
                dve.tensor_tensor(y[:, j], ps_y[j % 2][:, 0:D], y_low[:, j % 2], ALU.add).then_inc(y_done, 1)

            def dve_round(r, first=False, last=False):
                count = LAST if last else RING
                for j in range(count):
                    b = RING * r + j
                    if not (last and j + 2 >= count):
                        low_part_xT(b + 2, j % 2)
                    low_part_hT(b, j % 2)
                    if j + AHEAD < count:
                        if first:
                            set_source(0, j + AHEAD)
                        else:
                            set_source(r, j + AHEAD)
                    elif not last:
                        set_source(r + 1, j + AHEAD - RING)
                    if not (first and j == 0):
                        evacuate_y(*((r, j - 1) if j else (r - 1, RING - 1)))

            for j in range(AHEAD):
                set_source(0, j)
            for s in range(1 + PARTS, GROUPS - 1):
                add_shared(s)
            low_part_xT(0, 0)
            low_part_xT(1, 1)
            dve_round(0, first=True)
            with dve.Fori(1, ROUNDS - 1) as r:
                dve_round(r)
            dve_round(ROUNDS - 1, last=True)
            evacuate_y(ROUNDS - 1, LAST - 1)

            dve.wait_ge(gate_exp, 1)
            chained(dve.tensor_scalar(gate_d[:, :], gate_e[:, :], 1.0, None, ALU.add))
            chained(dve.reciprocal(gates[:, 0], gate_d[:, :]))
            chained(dve.tensor_tensor(gates[:, 1], gates[:, 0], gate_e[:, :], ALU.mult))
            dve.tensor_scalar(gates[:, :, :], gates[:, :, :], tanh_g[:, 1:2], None, ALU.mult).then_inc(gates_done, 1)
            dve.wait_ge(gates_done, 1)

            def combine(r, j):
                g = Y_SLOTS * r + j
                dve.wait_ge(y_loaded[j], 16 * K * (r + 1))
                hold(dve, counter)
                for t in range(G):
                    cols = ds(g * GW + t * D, D)
                    dve.scalar_tensor_tensor(out=xres[:, cols], in0=y_in[:, j, 0, t * D:(t + 1) * D],
                                             scalar=gates[:, 0, ds(g * G + t, 1)], in1=xres[:, cols],
                                             op0=ALU.mult, op1=ALU.add).then_inc(half_done, 1)

            with dve.Fori(0, GROUPS // Y_SLOTS - 1) as r:
                for j in range(Y_SLOTS):
                    combine(r, j)
            for j in range(Y_SLOTS):
                if j == Y_SLOTS - 1:
                    add_shared(GROUPS - 1)
                    dve.wait_ge(shared_done, GROUPS)
                combine(GROUPS // Y_SLOTS - 1, j)

        @block.tensor
        def _(pe):
            counter = pe_holds
            pe.wait_ge(consts_ready, 1)

            def matmul3(ps, aH, aL, bH, bL, start, stop):
                pe.matmul(ps, aH, bH, start=start, stop=False)
                pe.matmul(ps, aH, bL, start=False, stop=False)
                return pe.matmul(ps, aL, bH, start=False, stop=stop)

            def transpose_k(qq, j):
                g = 2 * qq + j
                pe.wait_ge(ctx_loaded[j], 16 * (qq + 1))
                at_least(pe, kT_done, g)
                for t in range(G):
                    last = pe.transpose(ps_k[:, t * P:(t + 1) * P], ctx_in[:, j, t * D:(t + 1) * D], ident[:, :])
                last.then_inc(kT_psum, 1)

            def score(qq, j):
                g = 2 * qq + j
                pe.wait_ge(kT_done, g + 1)
                if isinstance(qq, int) and g == 0:
                    pe.wait_ge(consts_ready, 2)
                at_least(pe, scores_done, g)
                pe.matmul(ps_s[:, :], ident4[:, 0], ident4[:, :, :].rearrange("p t d -> p (t d)"), start=True, stop=False,
                          skip_group_check=True)
                for t in range(G):
                    k_t = kT[:, j, t * P:(t + 1) * P]
                    last = pe.matmul(ps_s[:, t * P:(t + 1) * P], k_t, k_t, start=False, stop=(t == G - 1),
                                     skip_group_check=True)
                last.then_inc(s_psum, 1)

            def apply_scores(qq, j):
                g = 2 * qq + j
                pe.wait_ge(scores_done, g + 1)
                pe.wait_ge(q_done, g + 1)
                at_least(pe, x1_done, g)
                for t in range(G):
                    cols = slice(t * P, (t + 1) * P)
                    last = pe.matmul(ps_q[:, cols], scores[:, j, cols], q[:, j, cols], start=True, stop=True)
                last.then_inc(attn_psum, 1)

            def transpose_n(qq, j):
                g = 2 * qq + j
                pe.wait_ge(n_done, G * (g + 1))
                at_least(pe, nTL_done, g)
                for t in range(G):
                    last = pe.transpose(ps_n[:, t * P:(t + 1) * P], n[:, j, t * D:(t + 1) * D], ident[:, :])
                last.then_inc(nT_psum, 1)

            def transpose_weights(i):
                part_units = 2 * E // WEIGHT_PARTS
                if i == 0:
                    pe.wait_ge(w_loaded[0], 32)
                elif (i - 2) % part_units == 0:
                    pe.wait_ge(w_loaded[1 + (i - 2) // part_units], 32)
                at_least(pe, wL_done, i - 2)
                e = (i // 2 + E) % (E + 1)
                for c in range(HC):
                    w_in = (w1_in, w2_in)[i % 2][:, e * H + c * P:e * H + (c + 1) * P]
                    last = pe.transpose(ps_w[i % 3][:, c * P:(c + 1) * P], w_in, ident[:, :])
                last.then_inc(w_psum, 1)

            def logits_of(t):
                cols = slice(t * P, (t + 1) * P)
                both = ps_logit[:, t * 2 * E:(t + 1) * 2 * E]
                gate = gT[:, :, :].rearrange("p k e -> p (k e)")
                pe.matmul(both, nTH[:, cols], gate, start=True, stop=False)
                return pe.matmul(both, nTL[:, cols], gate, start=False, stop=True)

            def group_logits(g):
                pe.wait_ge(nTL_done, g + 1)
                for t in range(g * G, (g + 1) * G):
                    last = logits_of(t)
                last.then_inc(logit_psum, 1)

            def weights_early(i):
                for unit in range(EARLY):
                    transpose_weights(EARLY * i + unit)
                    if unit < 3 and 3 * i + unit < GROUPS - 3:
                        group_logits(3 * i + unit)
                if i >= 2:
                    group_logits(GROUPS - 5 + i)

            def weights_or_gate(i):
                if i == 0:
                    pe.wait_ge(route, 2)
                weights_early(i)

            def transpose_gate(half, j):
                if isinstance(half, int) and half == 1 and j == 1:
                    pe.wait_ge(small_in, 48)
                    pe.transpose(ps_gate[:, 0:E], gate_in[:, :], ident[0:E, 0:E]).then_inc(gate_psum, 1)


            run_phase_a(pe, (2, apply_scores), (1, score), (0, transpose_k), (4, transpose_n),
                        (0, transpose_gate), (TAIL, weights_or_gate))

            for unit in range(EARLY * LAGS, UNITS):
                transpose_weights(unit)
            group_logits(GROUPS - 1)

            def shared_up(s, c):
                i = HC * s + c
                at_least(pe, sT_done, i - HC + 1)
                hold(pe, counter)
                w = slice(E * H + c * P, E * H + (c + 1) * P)
                tokens = ds(s * GW, GW)
                matmul3(ps_sup[c][:, :], w1H[:, w], w1L[:, w], nTH[:, tokens], nTL[:, tokens],
                        start=True, stop=True).then_inc(sup_psum, 1)

            def shared_down(s, c, parity):
                i = HC * s + c
                if c == 0:
                    at_least(pe, sout_done, s - 1)
                pe.wait_ge(sTL_done, i + 1)
                w = w2[:, E * HC + c]
                last = matmul3(ps_sout[parity][:, :], w[:, 0], w[:, 1], sTH[c], sTL[c],
                               start=(c == 0), stop=(c == HC - 1))
                last.then_inc(sdown_done, 1)

            def shared_rows_back(s):
                pe.wait_ge(sout_done, s + 1)
                at_least(pe, shared_done, s)
                for t in range(G):
                    cols = slice(t * P, (t + 1) * P)
                    last = pe.transpose(ps_srows[:, cols], shared_T[:, cols], ident[:, :])
                last.then_inc(srows_psum, 1)

            pe.wait_ge(wL_done, UNITS)
            def prefix_counts():
                pe.wait_ge(picked_done, 1)
                by_expert = picked[:, :, :].rearrange("p t e -> p e t")
                pe.matmul(ps_before.rearrange("p (e t) -> p e t", e=E), before[:, :], by_expert, start=True, stop=True)
                pe.matmul(ps_total.rearrange("p (e t) -> p e t", e=E), ones[:, :], by_expert, start=True, stop=True)\
                    .then_inc(prefix_psum, 1)

            def invert(part):
                pe.wait_ge(onehot_done, part + 1)
                for i in range(part * PAIRS, (part + 1) * PAIRS):
                    last = pe.matmul(ps_inverse[:, 0:2 * BLOCKS], at_lane[:, i], at_block[:, i], start=(i == 0),
                                     stop=(i == K * TILES - 1))
                if part == PARTS - 1:
                    last.then_inc(inverse_psum, 1)

            def invert_half(half):
                for part in range(half * PARTS // 2, (half + 1) * PARTS // 2):
                    invert(part)

            run_shared(pe, shared_up, shared_down, shared_rows_back, prefix_counts, invert_half)
            pe.wait_ge(tables_done, 1)

            def transpose_rows(r, j):
                b = RING * r + j
                pe.wait_ge(gathered[j], 16 * (r + 1))
                at_least(pe, xTL_done, b - 1)
                pe.transpose(ps_x[j % 2][:, 0:P], rows_in[:, j], ident[:, :]).then_inc(xT_psum, 1)

            weight_reg = [pe.alloc_register(f"weight_reg{i}") for i in range(4)]

            def set_weights(r, j):
                pe.reg_load(weight_reg[j % 4], weight_at[0:1, ds(RING * r + j, 1)])

            def weight_start(j):
                return pe.snap(weight_reg[j % 4], min_val=0, max_val=(E - 1) * H)

            def up(b, j):
                at, slot2 = weight_start(j), j % 2
                pe.wait_ge(xTL_done, b + 1)
                at_least(pe, h_done, b - 1)
                hold(pe, counter)
                matmul3(ps_up[slot2][:, :], xTH[:, slot2], xTL[:, slot2], w1H[:, ds(at, H)], w1L[:, ds(at, H)],
                        start=True, stop=True).then_inc(up_psum, 1)

            def transpose_h(b, slot2):
                pe.wait_ge(h_done, b + 1)
                at_least(pe, hTL_done, b - 1)
                for c in range(HC):
                    cols = slice(c * P, (c + 1) * P)
                    last = pe.transpose(ps_hT[slot2][:, cols], h[:, slot2, cols], ident[:, :])
                last.then_inc(hT_psum, 1)

            def down(b, j):
                at, slot2 = weight_start(j), j % 2
                pe.wait_ge(hTL_done, b + 1)
                at_least(pe, y_done, b - 1)
                hold(pe, counter)
                for c in range(HC):
                    cols = slice(c * P, (c + 1) * P)
                    chunk = w2[:, :, :, :].rearrange("p c k d -> p (c k d)")[:, ds(2 * at + c * 2 * D, 2 * D)]
                    pe.matmul(ps_y[slot2][:, 0:2 * D], hTH[:, slot2, cols], chunk, start=(c == 0), stop=False)
                    last = pe.matmul(ps_y[slot2][:, 0:2 * D], hTL[:, slot2, cols], chunk, start=False,
                                     stop=(c == HC - 1))
                last.then_inc(y_psum, 1)

            def pe_round(r, first=False, last=False):
                count = LAST if last else RING
                for j in range(count):
                    b = RING * r + j
                    if not (last and j + 2 >= count):
                        transpose_rows(*((r, j + 2) if j + 2 < RING else (r + 1, j + 2 - RING)))
                    if not (last and j + 1 >= count):
                        up(b + 1, j + 1)
                    transpose_h(b, j % 2)
                    if not (first and j == 0):
                        down(b - 1, j - 1)
                    if not (last and j + 2 >= count):
                        set_weights(*((r, j + 2) if j + 2 < RING else (r + 1, j + 2 - RING)))

            transpose_rows(0, 0)
            transpose_rows(0, 1)
            set_weights(0, 0)
            set_weights(0, 1)
            pe.wait_ge(shared_done, GROUPS - 1)
            up(0, 0)
            pe_round(0, first=True)
            with pe.Fori(1, ROUNDS - 1) as r:
                pe_round(r)
            pe_round(ROUNDS - 1, last=True)
            down(USED - 1, LAST - 1)

            pe.wait_ge(y_done, USED)
            run_last_shared(shared_up, shared_down, shared_rows_back)


_INS = ["x", "ctx_1024", "g_xattn", "g_ffn", "L0_ffn_shared_w1", "L0_ffn_shared_w2", "L0_ffn_experts_w1",
        "L0_ffn_experts_w2", "L0_ffn_gate_w"]


def kernel(**inputs):
    import numpy as np
    import concourse.bacc as bacc
    from concourse.bass_utils import run_bass_kernel_spmd

    nc = bacc.Bacc("TRN2", target_bir_lowering=False, num_devices=1)
    arrays, args = {}, []
    for name in _INS:
        a = np.ascontiguousarray(inputs[name])
        arrays[f"in_{name}"] = a
        args.append(nc.dram_tensor(f"in_{name}", a.shape, mybir.dt.from_np(a.dtype), kind="ExternalInput").ap())
    out = nc.dram_tensor("out", inputs["x"].shape, mybir.dt.float32, kind="ExternalOutput").ap()
    flamingo_gated_moe(nc, *args, out)
    r = run_bass_kernel_spmd(nc, [arrays], core_ids=[0])
    return r.results[0]["out"]
```
